# Optimizing a Trainium2 kernel written in Bass

```python
import numpy as np
import jax
import jax.numpy as jnp

def _softmax(x, axis=-1):
    return jax.nn.softmax(x, axis=axis)

def _gelu(x):
    return jax.nn.gelu(x, approximate=True)

def _silu(x):
    return jax.nn.silu(x)

def _sigmoid(x):
    return jax.nn.sigmoid(x)

def _layernorm(x, axis=-1, eps=1e-05):
    m = jnp.mean(x, axis=axis, keepdims=True)
    v = jnp.var(x, axis=axis, keepdims=True)
    return (x - m) / jnp.sqrt(v + eps)

def _scatter_add(tgt, idx, src, axis=0):
    return tgt.at[idx].add(src)

def _segment_sum(src, seg, n):
    return jax.ops.segment_sum(src, seg, n)
kernel_name = 'mk_adj_resnorm_d4_adj_r2_e405dd'

def setup_inputs(seed: int=0):
    np.random.seed(seed)
    _w = jnp.asarray

    def _rec_inputs():
        import jax
        import jax.numpy as jnp
        _gk = jax.random.key(seed)
        x = -8.015e-05 + 0.9999 * jax.random.normal(jax.random.fold_in(_gk, 1), (128, 128, 128), jnp.float32)
        _w = (1.0 + jnp.arange(128, dtype=jnp.float32)) ** (-0.5)
        _w = _w / _w.mean()
        _pij = jnp.clip(0.0625 * _w[:, None] * _w[None, :], 0.0, 1.0)
        _a = jax.random.uniform(jax.random.fold_in(_gk, 2), (128, 128, 128)) < _pij
        _a = jnp.logical_or(_a, jnp.swapaxes(_a, -1, -2))
        _a = jnp.logical_or(_a, jnp.eye(128, dtype=bool))
        _af = _a.astype(jnp.float32)
        _af = _af * jax.random.uniform(jax.random.fold_in(_gk, 3), (128, 128, 128), jnp.float32, 0.05, 0.999837)
        adj = _af
        _nm = jnp.ones((128, 128), dtype=bool)
        nodemask = jnp.where(_nm, 1.0, 0.0).astype(jnp.float32)
        return (x, adj, nodemask)
    x, adj, nodemask = _rec_inputs()

    def _L0_gnn_setup():
        import jax, jax.numpy as jnp
        import numpy as np
        GROUPS = [list(range(25)), [0, 1, 2, 3, 4, 5, 6, 7, 8], [0, 9, 10, 11, 12, 13, 14], [6, 7, 8, 12, 13, 14], [3, 4, 5, 9, 10, 11]]
        B, N, D_IN, D_HID = (4096, 25, 128, 256)

        def _graph_conv(x, adj, W, b):
            n = adj.shape[-1]
            A = adj + jnp.eye(n, dtype=adj.dtype)
            deg = jnp.sum(A, axis=-1)
            deg_safe = jnp.where(deg == 0, 1.0, deg)
            dinv = jnp.where(deg == 0, 0.0, deg_safe ** (-0.5))
            norm_adj = dinv[:, :, None] * A * dinv[:, None, :]
            support = jnp.einsum('bnd,de->bne', x, W)
            out = jnp.einsum('bnm,bme->bne', norm_adj, support) + b
            return jax.nn.relu(out)
        key = jax.random.key(seed)
        ks = jax.random.split(key, 7)
        s1 = float(np.sqrt(6.0 / (D_IN + D_HID)))
        s2 = float(np.sqrt(6.0 / (D_HID + D_IN)))
        return {'x': jax.random.normal(ks[0], (B, N, D_IN), dtype=jnp.float32), 'adj': jax.random.uniform(ks[1], (B, N, N), dtype=jnp.float32), 'W1': jax.random.uniform(ks[2], (5, D_IN, D_HID), jnp.float32, -s1, s1), 'b1': jnp.zeros((5, D_HID), dtype=jnp.float32), 'W2': jax.random.uniform(ks[3], (5, D_HID, D_IN), jnp.float32, -s2, s2), 'b2': jnp.zeros((5, D_IN), dtype=jnp.float32), 'fusion_w': jnp.ones((5,), dtype=jnp.float32)}
    _L0_gnn_all = _L0_gnn_setup()
    _L0_gnn_in = {k: v for k, v in _L0_gnn_all.items() if k in ('W1', 'b1', 'W2', 'b2', 'fusion_w')}
    del _L0_gnn_all

    def _L1_gnn_setup():
        import math
        import jax, jax.numpy as jnp
        import numpy as np
        HIDDEN = 128
        HEADS = 8
        HEAD_DIM = HIDDEN // HEADS
        key = jax.random.key(seed)
        ks = jax.random.split(key, 8)
        b, n = (2, 2048)
        node_state = jax.random.normal(ks[0], (b, n, HIDDEN), dtype=jnp.float32)
        adjacency = jax.random.uniform(ks[1], (b, n, n), dtype=jnp.float32)
        s = 1.0 / math.sqrt(HIDDEN)
        Wq = jax.random.uniform(ks[2], (HIDDEN, HIDDEN), jnp.float32, -s, s)
        Wk = jax.random.uniform(ks[3], (HIDDEN, HIDDEN), jnp.float32, -s, s)
        Wv = jax.random.uniform(ks[4], (HIDDEN, HIDDEN), jnp.float32, -s, s)
        Wo = jax.random.uniform(ks[5], (HIDDEN, HIDDEN), jnp.float32, -s, s)
        bo = jax.random.uniform(ks[6], (HIDDEN,), jnp.float32, -s, s)
        return {'node_state': node_state, 'adjacency': adjacency, 'Wq': Wq, 'Wk': Wk, 'Wv': Wv, 'Wo': Wo, 'bo': bo}
    _L1_gnn_all = _L1_gnn_setup()
    _L1_gnn_in = {k: v for k, v in _L1_gnn_all.items() if k in ('Wq', 'Wk', 'Wv', 'Wo', 'bo')}
    del _L1_gnn_all

    def _L2_gnn_setup():
        import jax, jax.numpy as jnp
        import numpy as np
        B, N, F_IN, F_OUT = (8, 1024, 128, 128)
        key = jax.random.key(seed)
        k1, k2, k3, k4 = jax.random.split(key, 4)
        node_features = jax.random.normal(k1, (B, N, F_IN), dtype=jnp.float32)
        adj_matrix = jax.random.uniform(k2, (B, N, N), dtype=jnp.float32)
        lim = 1.0 / np.sqrt(F_IN)
        W = jax.random.uniform(k3, (F_OUT, F_IN), minval=-lim, maxval=lim, dtype=jnp.float32)
        b = jax.random.uniform(k4, (F_OUT,), minval=-lim, maxval=lim, dtype=jnp.float32)
        return {'node_features': node_features, 'adj_matrix': adj_matrix, 'W': W, 'b': b}
    _L2_gnn_all = _L2_gnn_setup()
    _L2_gnn_in = {k: v for k, v in _L2_gnn_all.items() if k in ('W', 'b')}
    del _L2_gnn_all

    def _L3_gnn_setup():
        import jax, jax.numpy as jnp
        import numpy as np
        B, N, D, C, L = (64, 256, 128, 128, 5)
        EDGE_P = 0.02

        def _gru_cell(m, h, w_ih, w_hh, b_ih, b_hh):
            gi = m @ w_ih.T + b_ih
            gh = h @ w_hh.T + b_hh
            i_r, i_z, i_n = jnp.split(gi, 3, axis=-1)
            h_r, h_z, h_n = jnp.split(gh, 3, axis=-1)
            r = jax.nn.sigmoid(i_r + h_r)
            z = jax.nn.sigmoid(i_z + h_z)
            n = jnp.tanh(i_n + r * h_n)
            return (1.0 - z) * n + z * h
        key = jax.random.key(seed)
        ks = jax.random.split(key, 8)
        x = jax.random.normal(ks[0], (B, N, D), dtype=jnp.float32)
        adj = (jax.random.uniform(ks[1], (B, N, N)) < EDGE_P).astype(jnp.float32)
        mask = jnp.ones((B, N), dtype=jnp.float32)
        s = 1.0 / np.sqrt(C).astype(np.float32)
        weight = jax.random.uniform(ks[2], (L, C, C), minval=-s, maxval=s, dtype=jnp.float32)
        w_ih = jax.random.uniform(ks[3], (3 * C, C), minval=-s, maxval=s, dtype=jnp.float32)
        w_hh = jax.random.uniform(ks[4], (3 * C, C), minval=-s, maxval=s, dtype=jnp.float32)
        b_ih = jax.random.uniform(ks[5], (3 * C,), minval=-s, maxval=s, dtype=jnp.float32)
        b_hh = jax.random.uniform(ks[6], (3 * C,), minval=-s, maxval=s, dtype=jnp.float32)
        return dict(x=x, adj=adj, mask=mask, weight=weight, w_ih=w_ih, w_hh=w_hh, b_ih=b_ih, b_hh=b_hh)
    _L3_gnn_all = _L3_gnn_setup()
    _L3_gnn_in = {k: v for k, v in _L3_gnn_all.items() if k in ('weight', 'w_ih', 'w_hh', 'b_ih', 'b_hh')}
    del _L3_gnn_all
    return {'x': x, 'adj': adj, 'nodemask': nodemask, 'L0_gnn_W1': _L0_gnn_in['W1'], 'L0_gnn_b1': _L0_gnn_in['b1'], 'L0_gnn_W2': _L0_gnn_in['W2'], 'L0_gnn_b2': _L0_gnn_in['b2'], 'L0_gnn_fusion_w': _L0_gnn_in['fusion_w'], 'L1_gnn_Wq': _L1_gnn_in['Wq'], 'L1_gnn_Wk': _L1_gnn_in['Wk'], 'L1_gnn_Wv': _L1_gnn_in['Wv'], 'L1_gnn_Wo': _L1_gnn_in['Wo'], 'L1_gnn_bo': _L1_gnn_in['bo'], 'L2_gnn_W': _L2_gnn_in['W'], 'L2_gnn_b': _L2_gnn_in['b'], 'L3_gnn_weight': _L3_gnn_in['weight'], 'L3_gnn_w_ih': _L3_gnn_in['w_ih'], 'L3_gnn_w_hh': _L3_gnn_in['w_hh'], 'L3_gnn_b_ih': _L3_gnn_in['b_ih'], 'L3_gnn_b_hh': _L3_gnn_in['b_hh']}

def reference(x, adj, nodemask, L0_gnn_W1, L0_gnn_b1, L0_gnn_W2, L0_gnn_b2, L0_gnn_fusion_w, L1_gnn_Wq, L1_gnn_Wk, L1_gnn_Wv, L1_gnn_Wo, L1_gnn_bo, L2_gnn_W, L2_gnn_b, L3_gnn_weight, L3_gnn_w_ih, L3_gnn_w_hh, L3_gnn_b_ih, L3_gnn_b_hh):
    import jax
    import jax.numpy as jnp

    def _L0_gnn_ref(x, adj, W1, b1, W2, b2, fusion_w):
        import jax, jax.numpy as jnp
        import numpy as np
        GROUPS = [list(range(25)), [0, 1, 2, 3, 4, 5, 6, 7, 8], [0, 9, 10, 11, 12, 13, 14], [6, 7, 8, 12, 13, 14], [3, 4, 5, 9, 10, 11]]
        B, N, D_IN, D_HID = (4096, 25, 128, 256)

        def _graph_conv(x, adj, W, b):
            n = adj.shape[-1]
            A = adj + jnp.eye(n, dtype=adj.dtype)
            deg = jnp.sum(A, axis=-1)
            deg_safe = jnp.where(deg == 0, 1.0, deg)
            dinv = jnp.where(deg == 0, 0.0, deg_safe ** (-0.5))
            norm_adj = dinv[:, :, None] * A * dinv[:, None, :]
            support = jnp.einsum('bnd,de->bne', x, W)
            out = jnp.einsum('bnm,bme->bne', norm_adj, support) + b
            return jax.nn.relu(out)
        norm_w = jax.nn.softmax(fusion_w)
        fused = jnp.zeros_like(x)
        for g, idx_list in enumerate(GROUPS):
            idx = jnp.asarray(idx_list)
            x_g = x[:, idx, :]
            adj_g = adj[:, idx][:, :, idx]
            h = _graph_conv(x_g, adj_g, W1[g], b1[g])
            out_g = _graph_conv(h, adj_g, W2[g], b2[g])
            fused = fused.at[:, idx, :].add(norm_w[g] * out_g)
        return fused

    def _L1_gnn_ref(node_state, adjacency, Wq, Wk, Wv, Wo, bo):
        import math
        import jax, jax.numpy as jnp
        import numpy as np
        HIDDEN = 128
        HEADS = 8
        HEAD_DIM = HIDDEN // HEADS
        b, n, _ = node_state.shape

        def split_heads(x):
            return x.reshape(b, n, HEADS, HEAD_DIM).transpose(0, 2, 1, 3)
        q = split_heads(node_state @ Wq.T)
        k = split_heads(node_state @ Wk.T)
        v = split_heads(node_state @ Wv.T)
        scores = jnp.einsum('bhqd,bhkd->bhqk', q, k) / math.sqrt(HEAD_DIM)
        log_adj = jnp.log(adjacency + 1e-06)
        scores = scores + log_adj[:, None, :, :]
        attn = jax.nn.softmax(scores, axis=-1)
        out = jnp.einsum('bhqk,bhkd->bhqd', attn, v)
        out = out.transpose(0, 2, 1, 3).reshape(b, n, HIDDEN)
        return out @ Wo.T + bo

    def _L2_gnn_ref(node_features, adj_matrix, W, b):
        import jax, jax.numpy as jnp
        import numpy as np
        B, N, F_IN, F_OUT = (8, 1024, 128, 128)
        degree = jnp.sum(adj_matrix, axis=-1)
        d_inv_sqrt = jnp.power(degree, -0.5)
        d_inv_sqrt = jnp.where(jnp.isinf(d_inv_sqrt), 0.0, d_inv_sqrt)
        norm_adj = adj_matrix * d_inv_sqrt[:, :, None] * d_inv_sqrt[:, None, :]
        transformed = jnp.einsum('bnf,of->bno', node_features, W) + b
        output = jnp.einsum('bnm,bmo->bno', norm_adj, transformed)
        return jax.nn.relu(output)

    def _L3_gnn_ref(x, adj, mask, weight, w_ih, w_hh, b_ih, b_hh):
        import jax, jax.numpy as jnp
        import numpy as np
        B, N, D, C, L = (64, 256, 128, 128, 5)
        EDGE_P = 0.02

        def _gru_cell(m, h, w_ih, w_hh, b_ih, b_hh):
            gi = m @ w_ih.T + b_ih
            gh = h @ w_hh.T + b_hh
            i_r, i_z, i_n = jnp.split(gi, 3, axis=-1)
            h_r, h_z, h_n = jnp.split(gh, 3, axis=-1)
            r = jax.nn.sigmoid(i_r + h_r)
            z = jax.nn.sigmoid(i_z + h_z)
            n = jnp.tanh(i_n + r * h_n)
            return (1.0 - z) * n + z * h
        A = (adj != 0).astype(x.dtype)
        h = x
        for l in range(weight.shape[0]):
            m = jnp.einsum('bnd,de->bne', h, weight[l])
            agg = jnp.einsum('bij,bid->bjd', A, m)
            h = _gru_cell(agg, h, w_ih, w_hh, b_ih, b_hh)
        return h * mask[..., None]
    x = _layernorm(x + _L0_gnn_ref(x, adj, L0_gnn_W1, L0_gnn_b1, L0_gnn_W2, L0_gnn_b2, L0_gnn_fusion_w), axis=-1)
    x = _layernorm(x + _L1_gnn_ref(x, adj, L1_gnn_Wq, L1_gnn_Wk, L1_gnn_Wv, L1_gnn_Wo, L1_gnn_bo), axis=-1)
    x = _layernorm(x + _L2_gnn_ref(x, adj, L2_gnn_W, L2_gnn_b), axis=-1)
    x = _layernorm(x + _L3_gnn_ref(x, adj, nodemask, L3_gnn_weight, L3_gnn_w_ih, L3_gnn_w_hh, L3_gnn_b_ih, L3_gnn_b_hh), axis=-1)
    return x

_drawn_inputs = setup_inputs


def setup_inputs(seed=0):
    import zlib

    import numpy as np

    out = dict(_drawn_inputs(seed))
    spreads = {'L0_gnn_b1': (0.0, 0.1), 'L0_gnn_b2': (0.0, 0.1), 'L0_gnn_fusion_w': (1.0, 0.2)}
    factors = {}
    for name, (base, spread) in spreads.items():
        noise = np.random.default_rng([zlib.crc32(name.encode()), seed]).standard_normal(out[name].shape)
        drawn = base * np.exp(spread * noise) if base else spread * noise
        out[name] = jnp.asarray(drawn.astype(out[name].dtype))
    for name, factor in factors.items():
        out[name] = (out[name] * factor).astype(out[name].dtype)
    return out
```

```python
from contextlib import ExitStack

import concourse.bass as bass
from concourse import mybir

F32 = mybir.dt.float32
ALU = mybir.AluOpType
ACT = mybir.ActivationFunctionType
AX_X = mybir.AxisListType.X

P = 128
GB = 4
NG = 2
W = GB * P
HEADS, DH = 8, 16
NN, NS = 25, 32
GROUPS = [list(range(25)), [0, 1, 2, 3, 4, 5, 6, 7, 8], [0, 9, 10, 11, 12, 13, 14],
          [6, 7, 8, 12, 13, 14], [3, 4, 5, 9, 10, 11]]
NK = len(GROUPS)
LAYERS = 5
LN_EPS, ADJ_EPS = 1e-5, 1e-6
SCALE = float(DH) ** -0.5

PER = dict(
    l0_prep=10 * NG, l0_pow=NG, y_mm=NG, y_t=NG, w1_mm=2 * NG, hid_t=2 * NG, z_mm=2 * NG, z_lo=NG, z_hi=NG,
    o_mm=NG, o_relu=NG, fused=2 * NG, fused_mm=NG, y1=NG,
    ln1=3 * NG, ln1_pow=NG, ln2=3 * NG, ln2_pow=NG, ln3=3 * NG, ln3_pow=NG, x1=NG, x2=NG,
    adjt_mm=NG, adj_t=NG, adj_te=NG, x1t_mm=NG, x1_t=NG, x1_b=NG, k_mm=NG, q_mm=NG, v_mm=NG, k_t=NG, q_t=NG, v_p=NG,
    s_mm=GB * NG, s_max=GB * NG, s_neg=GB * NG, e_act=2 * GB * NG, et_mm=2 * GB * NG, p_t=2 * GB * NG,
    av_mm=GB * NG, o_t=2 * NG, u_mm=2 * NG, den=2 * NG, o_n=2 * NG, ont_mm=2 * NG, on_t=2 * NG, wo_mm=2 * NG, y2=2 * NG,
    deg=3 * NG, deg_pow=NG, dinv=NG, x2t_mm=NG, x2_t=NG, t_mm=NG, t_b=NG, t_d=NG, a_mm=NG, a_relu=NG, y3=NG,
)
PER_GRU = dict(
    a_bin=1, x3=1, x3t_mm=1, h_first=1, h_mm=LAYERS - 1, h_tok=LAYERS - 1,
    agg_mm=LAYERS, agg_t=LAYERS, r_mm=LAYERS, hn_mm=LAYERS, in_mm=LAYERS, zg_mm=LAYERS,
    r_act=LAYERS, u_act=LAYERS, n_act=LAYERS, z_act=LAYERS, rv=LAYERS, rw=LAYERS, hd=LAYERS, he=LAYERS, h_new=LAYERS,
    f_mm=1, y4=1, ln4=3, ln4_pow=1, x4=1,
)
LAG = 3



def attention_steps(half):
    at = (1, half)
    out = [(*at, "x1", 0, 2), (*at, "x1_t", 0, 2), (*at, "qkv", 0, 7)]
    for b in range(GB):
        out += [(*at, "s", b, 4), (*at, "t", b, 3)]
        if b == 2:
            out += [(*at, "on", 0, 2), (*at, "wo", 0, 1)]
        out += [(*at, "a", b, 1)]
        if b == 1:
            out += [(*at, "u", 0, 1)]
    return out + [(*at, "u", 1, 2), (*at, "on", 1, 2), (*at, "wo", 1, 2)]


def first_third_steps(half):
    end, last, start = (1 - half, 1 - half), (2 - half, 1 - half), (0, half)
    return [(*end, "l0_z", 0, 2), (*end, "l0_z", 1, 2), (*end, "l0_out", 0, 2),
            (*last, "x2", 0, 1), (*last, "x2_t", 0, 2), (*last, "l2_t", 0, 4), (*last, "l2_agg", 0, 3),
            (*end, "adj_t", 0, 2), (*end, "l0_add", 0, 3),
            (*start, "l0_prep", 0, 4), (*start, "l0_y", 0, 2), (*start, "l0_hid", 0, 3), (*start, "l0_hid", 1, 3)]


def gated_steps(half):
    this, other, new = (2, half), (3 - half, 1 - half), (2 - half, 1 - half)
    out = []
    for at, layer in ((this, 0), (other, 3), (this, 1), (other, 4), (this, 2)):
        if at == this and layer == 2:
            out += [(*other, "end", 0, 1), (*new, "bin", 0, 0)]
        out += [(*at, kind, layer, t) for kind, t in
                (("turn", 1), ("agg", 2), ("r", 2), ("hn", 1), ("in", 1), ("z", 2))]
    return out[:-1] + [(*new, "x3", 0, 0), out[-1], (*new, "begin", 0, 1)]


def body_steps():
    out = []
    for half in range(NG):
        timed = []
        for n, (thread, steps) in enumerate((("A", attention_steps(half)), ("B", first_third_steps(half)), ("R", gated_steps(half)))):
            total, at = sum(s[-1] for s in steps), 0
            for s in steps:
                timed.append((at / total, n, len(timed), thread, s[:-1]))
                at += s[-1]
        out += [(thread, *s) for _, _, _, thread, s in sorted(timed)]
    return out


BODY = body_steps()
SLOTS = [(g, k) for thread, _, g, kind, k in BODY if kind == "agg"]
BEFORE = {slot: SLOTS[n - 1] for n, slot in enumerate(SLOTS)}
LAG_OF = {(g, k): lag for thread, lag, g, kind, k in BODY if kind == "agg"}


def gnn_stack_kernel(nc, x, adj, nodemask, W1, b1, W2, b2, fusion_w, Wq, Wk, Wv, Wo, bo, L2W, L2b,
                     Wl, w_ih, w_hh, b_ih, b_hh, out):
    NB = x.shape[0]
    ITERS = NB // (GB * NG)
    with ExitStack() as ctx:
        def sb(name, shape, dt=F32):
            return ctx.enter_context(nc.sbuf_tensor(name, shape, dt))

        def sem(name):
            return ctx.enter_context(nc.semaphore(name))

        S = {name: sem(name) for name in PER}
        SG = {name: [sem(f"{name}_g{g}") for g in range(NG)] for name in PER_GRU}
        consts_ready, w_in, w_prep, w_mm, w_evac = (sem(n) for n in ("consts_ready", "w_in", "w_prep", "w_mm", "w_evac"))
        wait_over = sem("wait_over")
        w_exp, w_pool = sem("w_exp"), sem("w_pool")
        x_in = [sem(f"x_in{g}") for g in range(NG)]
        small_in = [sem(f"small_in{g}") for g in range(NG)]
        adj_in = [sem(f"adj_in{g}") for g in range(NG)]
        adjr_in = [sem(f"adjr_in{g}") for g in range(NG)]
        km_in = [sem(f"km_in{g}") for g in range(NG)]
        out_done = [sem(f"out_done{g}") for g in range(NG)]

        def wait(eng, name, it, k):
            eng.wait_ge(S[name], it * PER[name] + k)

        def wait_g(eng, name, g, it, k):
            eng.wait_ge(SG[name][g], it * PER_GRU[name] + k)

        def passed(eng):
            eng.sem_inc(wait_over, 1)

        def program(eng, steps):
            def iteration(it, some):
                for thread, lag, g, kind, k in BODY:
                    if not some or 0 <= it - lag < ITERS:
                        steps(it - lag, g, kind, k)

            for it in range(LAG):
                iteration(it, True)
            with eng.Fori(LAG, ITERS) as it:
                iteration(it, False)
            for it in range(ITERS, ITERS + LAG):
                iteration(it, True)

        ident = sb("ident", [P, P])
        ident_small = sb("ident_small", [P, NS])
        member = sb("member", [P, NK, NS])
        member_p = sb("member_p", [P, NK])
        member_x = sb("member_x", [P, NK, NS])
        half_neg = sb("half_neg", [P, NK])
        stage = sb("stage", [P, 18, P])
        wT = sb("wT", [P, 18, P])
        WQ, WK, WV, WO, WL2, WHH, WIH, WL, MASK, BIAS = 0, 1, 2, 3, 4, 5, 8, 11, 16, 17
        whn = sb("whn", [P, P])
        comp = sb("comp", [P, LAYERS, 3 * P])
        W1s = sb("W1s", [P, NK, 2 * P])
        W2s = sb("W2s", [P, NK, 2, P])
        b1c = wT[:, BIAS, 0:2 * NK].rearrange("p (g h) -> p g h", h=2)
        b2c = wT[:, BIAS, 2 * NK:3 * NK]
        fw = sb("fw", [P, NK])
        fwx = sb("fwx", [P, NK])
        fw_s = sb("fw_s", [P, 4])
        fusion = sb("fusion", [P, NK])
        fusion_b2 = sb("fusion_b2", [P, NK])
        bih = wT[:, BIAS, 15:18]
        bhh = wT[:, BIAS, 18:21]
        b_rz = sb("b_rz", [P, 3])
        b_hn = sb("b_hn", [P, 1])
        bo_row = sb("bo_row", [P, P])
        l2b_row = sb("l2b_row", [P, P])

        xin = [sb(f"xin_{g}", [P, GB, P]) for g in range(NG)]
        xs = [sb(f"xs_{g}", [P, P]) for g in range(NG)]
        adjc = [sb(f"adjc_{g}", [P, NS]) for g in range(NG)]
        adjn = [sb("adjn", [P, GB, P])] * NG
        adjr = [sb(f"adjr_{g}", [P, GB, P]) for g in range(NG)]
        a_i = sb("a_i", [P, NS])
        a_m = sb("a_m", [P, NK, NS])
        deg0 = sb("deg0", [P, NK])
        deg0_z = sb("deg0_z", [P, NK])
        deg0_s = sb("deg0_s", [P, NK])
        pow0 = sb("pow0", [P, NK])
        dinv0 = sb("dinv0", [P, NK])
        dinv0m = sb("dinv0m", [P, NK])
        a_row = sb("a_row", [P, NK, NS])
        a_col = sb("a_col", [P, NK, NS])
        nat = sb("nat", [P, NK, GB, NN])
        y_t = sb("y_t", [P, NK, GB, NN])
        hid_t = sb("hid_t", [P, 2, NK, GB, NS])
        z_s = sb("z_s", [P, NK, P])
        o_r = sb("o_r", [P, NK, GB, NN])
        o_m = sb("o_m", [P, NK, GB, NN])
        f_t = sb("f_t", [P, GB * NN])
        stats = [sb(f"stats_{j}", [P, GB, 6]) for j in range(3)]
        mv = [[sb(f"mv_{g}{j}", [P, GB, 2]) for j in range(3)] for g in range(NG)]
        ve = [[sb(f"ve_{g}{j}", [P, GB]) for j in range(3)] for g in range(NG)]
        rs = [[sb(f"rs_{g}{j}", [P, GB]) for j in range(3)] for g in range(NG)]
        x1 = [sb("x1", [P, GB, P])] * NG
        x1b = [sb("x1b", [P, GB, P])] * NG
        x2 = [sb("x2", [P, GB, P])] * NG
        y2 = [sb(f"y2_{g}", [P, GB, P]) for g in range(NG)]
        y3 = [sb(f"y3_{g}", [P, GB, P]) for g in range(NG)]
        adjT = [sb(f"adjT_{g}", [P, GB, P]) for g in range(NG)]
        adjTe = [sb("adjTe", [P, GB, P])] * NG
        xT = [sb("xT", [P, GB, P])] * NG
        x2T = [sb("x2T", [P, GB, P])] * NG
        kT = [sb("kT", [P, GB, P])] * NG
        qT = [sb("qT", [P, GB, P])] * NG
        km = [sb(f"km_{g}", [P, GB, HEADS, P]) for g in range(NG)]
        vp = [sb("vp", [P, GB, HEADS, NS])] * NG
        s_mx = sb("s_mx", [P, HEADS])
        s_ng = sb("s_ng", [P, HEADS])
        e_s = sb("e_s", [P, HEADS, P])
        p_s = sb("p_s", [P, HEADS, P])
        o_ts = sb("o_ts", [P, 2, 2, P])
        den = sb("den", [P, 2, HEADS])
        o_ns = sb("o_ns", [P, 2, HEADS, DH])
        on_ts = sb("on_ts", [P, 2, P])
        deg = [sb(f"deg_{g}", [P, GB]) for g in range(NG)]
        deg_z = [sb(f"deg_z_{g}", [P, GB]) for g in range(NG)]
        deg_s = [sb(f"deg_s_{g}", [P, GB]) for g in range(NG)]
        deg_p = [sb(f"deg_p_{g}", [P, GB]) for g in range(NG)]
        dinv = [sb(f"dinv_{g}", [P, GB]) for g in range(NG)]
        t_b = sb("t_b", [P, GB, P])
        t_d = sb("t_d", [P, GB, P])
        a_r = sb("a_r", [P, GB, P])

        x3 = [sb(f"x3_{g}", [P, GB, P]) for g in range(NG)]
        a_bin = [sb(f"a_bin_{g}", [P, GB, P]) for g in range(NG)]
        hT = [sb(f"hT_{g}", [P, W]) for g in range(NG)]
        h_tok = [sb(f"h_tok_{g}", [P, GB, P]) for g in range(NG)]
        agg = [sb(f"agg_{g}", [P, W]) for g in range(NG)]
        tr = [sb(f"tr_{g}", [P, W]) for g in range(NG)]
        tz = [sb(f"tz_{g}", [P, W]) for g in range(NG)]
        un = [sb(f"un_{g}", [P, W]) for g in range(NG)]
        nn = [sb(f"nn_{g}", [P, W]) for g in range(NG)]
        hd = [sb(f"hd_{g}", [P, W]) for g in range(NG)]
        y4 = [sb(f"y4_{g}", [P, GB, P]) for g in range(NG)]
        x4 = [sb(f"x4_{g}", [P, GB, P]) for g in range(NG)]
        stats4 = [sb(f"stats4_{g}", [P, GB, 6]) for g in range(NG)]
        mv4 = [sb(f"mv4_{g}", [P, GB, 2]) for g in range(NG)]
        ve4 = [sb(f"ve4_{g}", [P, GB]) for g in range(NG)]
        rs4 = [sb(f"rs4_{g}", [P, GB]) for g in range(NG)]

        def bank(name):
            return ctx.enter_context(nc.psum_tensor(name, [P, 512], F32))

        S0, S1, M0, M1, M2, RT, RA, RB = (bank(n) for n in ("S0", "S1", "M0", "M1", "M2", "RT", "RA", "RB"))

        def cols(t):
            return t[:, :, :].rearrange("p b d -> p (b d)")

        def per_graph(v):
            return v.unsqueeze(2).broadcast_to([P, GB, P])

        xr = x.rearrange("b n d -> n b d")
        ar = adj.rearrange("b n m -> n b m")
        outr = out.rearrange("b n d -> n b d")
        WEIGHT_DMAS = 5 + 1 + 1 + 1 + 1 + 1 + 2 + 4 + 2 + 1
        block = ctx.enter_context(nc.Block())

        @block.sync
        def _(sp):
            for i, w in enumerate((Wq, Wk, Wv, Wo, L2W)):
                sp.dma_start(stage[:, i, :], w).then_inc(w_in, 16)
            sp.dma_start(stage[:, WHH:WHH + 3, :], w_hh.rearrange("(c p) d -> p c d", p=P)).then_inc(w_in, 16)
            sp.dma_start(stage[:, WIH:WIH + 3, :], w_ih.rearrange("(c p) d -> p c d", p=P)).then_inc(w_in, 16)
            sp.dma_start(stage[:, WL:WL + LAYERS, :], Wl.rearrange("l c d -> c l d")).then_inc(w_in, 16)
            sp.dma_start(stage[:, MASK, :], nodemask).then_inc(w_in, 16)
            sp.dma_start(W1s[:, :, :], W1.rearrange("g d e -> d g e")).then_inc(w_in, 16)
            for h in range(2):
                sp.dma_start(W2s[:, :, h, :], W2[:, h * P:(h + 1) * P, :].rearrange("g e d -> e g d")).then_inc(w_in, 16)
            sp.wait_ge(w_pool, 1)
            sp.dma_start(stage[0:10, BIAS, :], b1.rearrange("g (h p) -> (g h) p", p=P)).then_inc(w_in, 16)
            sp.dma_start(stage[10:15, BIAS, :], b2).then_inc(w_in, 16)
            sp.dma_start(stage[15:18, BIAS, :], b_ih.rearrange("(c p) -> c p", p=P)).then_inc(w_in, 16)
            sp.dma_start(stage[18:21, BIAS, :], b_hh.rearrange("(c p) -> c p", p=P)).then_inc(w_in, 16)
            sp.dma_start(bo_row[:, :], bo.partition_broadcast(P)).then_inc(w_in, 16)
            sp.dma_start(l2b_row[:, :], L2b.partition_broadcast(P)).then_inc(w_in, 16)
            sp.dma_start(fw[:, :], fusion_w.partition_broadcast(P)).then_inc(w_in, 16)

            def load_small(g, it, again):
                b0 = it * (NG * GB) + g * GB
                for b in range(GB):
                    if again and b == 0:
                        wait(sp, "y_mm", it - 1, g + 1)
                    sp.dma_start(adjc[g][NS * b:NS * b + NS, :], adj[bass.ds(b0 + b, 1), 0:NS, 0:NS].rearrange("a n d -> (a n) d"))\
                        .then_inc(small_in[g], 16)
                    sp.dma_start(xs[g][NS * b:NS * b + NS, :], x[bass.ds(b0 + b, 1), 0:NS, :].rearrange("a n d -> (a n) d"))\
                        .then_inc(small_in[g], 16)

            def load(g, it, again):
                b0 = it * (NG * GB) + g * GB
                if g:
                    wait(sp, "adj_t", it, g)
                    wait(sp, "deg", it, 3 * g)
                elif again:
                    wait(sp, "adj_t", it - 1, NG)
                    wait(sp, "deg", it - 1, 3 * NG)
                sp.dma_start(adjn[g][:, :, :], ar[:, bass.ds(b0, GB), :]).then_inc(adj_in[g], 16)
                if again:
                    wait(sp, "x1", it - 1, g + 1)
                sp.dma_start(xin[g][:, :, :], xr[:, bass.ds(b0, GB), :]).then_inc(x_in[g], 16)

            def load_again(g, it, again):
                b0 = it * (NG * GB) + g * GB
                if again:
                    wait_g(sp, "a_bin", g, it - 1, 1)
                sp.dma_start(adjr[g][:, :, :], ar[:, bass.ds(b0, GB), :]).then_inc(adjr_in[g], 16)

            def spread_keys(g, it):
                wait(sp, "k_t", it, g + 1)
                for h in range(HEADS):
                    r = slice(DH * h, DH * h + DH)
                    sp.dma_start(km[g][r, :, h, :], kT[g][r, :, :]).then_inc(km_in[g], 16)

            def store(g, it):
                b0 = it * (NG * GB) + g * GB
                wait_g(sp, "x4", g, it, 1)
                sp.dma_start(outr[:, bass.ds(b0, GB), :], x4[g][:, :, :]).then_inc(out_done[g], 16)

            ORDER = [(0, 0, "small"), (1, 0, "keys"), (3, 0, "store"), (2, 1, "again"), (0, 0, "load"),
                     (0, 1, "small"), (1, 1, "keys"), (3, 1, "store"), (1, 0, "again"), (0, 1, "load")]

            def iteration(it, some):
                for lag, g, what in ORDER:
                    if some and not 0 <= it - lag < ITERS:
                        continue
                    n = it - lag
                    again = not (some and n == 0)
                    if what == "keys":
                        spread_keys(g, n)
                    elif what == "small":
                        load_small(g, n, again)
                    elif what == "load":
                        load(g, n, again)
                    elif what == "again":
                        load_again(g, n, again)
                    else:
                        store(g, n)

            for g in range(NG):
                sp.sem_inc(out_done[g], 16)
            for it in range(LAG):
                iteration(it, True)
            with sp.Fori(LAG, ITERS) as it:
                iteration(it, False)
            for it in range(ITERS, ITERS + LAG + 1):
                iteration(it, True)
            for g in range(NG):
                sp.wait_ge(out_done[g], 16 * (ITERS + 1))

        @block.gpsimd
        def _(pool):
            n = [0]

            def after(ins):
                n[0] += 1
                ins.then_inc(w_pool, 1)
                pool.wait_ge(w_pool, n[0])

            after(pool.memset(stage[:, BIAS, :], 0.0))
            after(pool.memset(ident[:, :], 0.0))
            after(pool.affine_select(out=ident[:, :], in_=ident[:, :], compare_op=ALU.not_equal, fill=1.0,
                                     base=0, pattern=[[-1, P]], channel_multiplier=1))
            after(pool.memset(member[:, :, :], 0.0))
            for c, nodes in enumerate(GROUPS):
                a = 0
                while a < len(nodes):
                    b = a
                    while b + 1 < len(nodes) and nodes[b + 1] == nodes[b] + 1:
                        b += 1
                    pool.memset(member[:, c, nodes[a]:nodes[b] + 1], 1.0)
                    a = b + 1
            for t in (nat, hid_t, vp[0], km[0], km[1]):
                after(pool.memset(t[tuple([slice(None)] * len(t.shape))], 0.0))
            pool.memset(vp[0][:, :, :, DH:DH + 1], 1.0)
            pool.memset(half_neg[:, :], -0.5).then_inc(consts_ready, 1)

            def root(v, r):
                return pool.tensor_tensor(r[:, :], v[:, :], half_neg[:, 0:GB], ALU.pow)

            def steps(it, g, kind, k):
                if kind == "l0_prep":
                    wait(pool, "l0_prep", it, 10 * g + 5)
                    pool.tensor_tensor(pow0[:, :], deg0_s[:, :], half_neg[:, :], ALU.pow).then_inc(S["l0_pow"], 1)
                elif kind == "l0_add":
                    wait(pool, "ln1", it, 3 * g + 3)
                    root(ve[g][0], rs[g][0]).then_inc(S["ln1_pow"], 1)
                elif kind == "adj_t":
                    wait(pool, "deg", it, 3 * g + 3)
                    root(deg_s[g], deg_p[g]).then_inc(S["deg_pow"], 1)
                elif kind == "x1":
                    wait(pool, "adj_t", it, g + 1)
                    passed(pool)
                    pool.tensor_scalar(cols(adjTe[g]), cols(adjT[g]), 1.0, ADJ_EPS, ALU.mult, ALU.add).then_inc(S["adj_te"], 1)
                elif kind == "x1_t":
                    wait(pool, "x1", it, g + 1)
                    pool.tensor_tensor(x1b[g][:, :, :], x1[g][:, :, :], bo_row[:, :].unsqueeze(1).broadcast_to([P, GB, P]), ALU.add)\
                        .then_inc(S["x1_b"], 1)
                elif kind == "wo" and k == 1:
                    wait(pool, "ln2", it, 3 * g + 3)
                    root(ve[g][1], rs[g][1]).then_inc(S["ln2_pow"], 1)
                elif kind == "l2_t":
                    wait(pool, "t_b", it, g + 1)
                    wait(pool, "dinv", it, g + 1)
                    pool.tensor_tensor(t_d[:, :, :], t_b[:, :, :], per_graph(dinv[g][:, :]), ALU.mult).then_inc(S["t_d"], 1)
                elif kind == "l2_agg":
                    wait(pool, "ln3", it, 3 * g + 3)
                    root(ve[g][2], rs[g][2]).then_inc(S["ln3_pow"], 1)
                elif kind == "z":
                    wait_g(pool, "n_act", g, it, k + 1)
                    pool.tensor_tensor(hd[g][:, :], hT[g][:, :], nn[g][:, :], ALU.subtract).then_inc(SG["hd"][g], 1)
                elif kind == "end":
                    wait_g(pool, "ln4", g, it, 3)
                    root(ve4[g], rs4[g]).then_inc(SG["ln4_pow"][g], 1)

            program(pool, steps)

        @block.scalar
        def _(act):
            act.wait_ge(w_prep, 2)
            act.activation(fw[:, :], fwx[:, :], ACT.Exp).then_inc(w_exp, 1)
            act.wait_ge(w_evac, 7)

            def steps(it, g, kind, k):
                n = GB * g + k
                if kind == "l0_y":
                    wait(act, "y_mm", it, g + 1)
                    act.activation(y_t[:, :, :, :].rearrange("p k b n -> p (k b n)"), M2[:, 0:NK * GB * NN], ACT.Copy).then_inc(S["y_t"], 1)
                elif kind == "l0_hid":
                    wait(act, "w1_mm", it, 2 * g + k + 1)
                    for c in range(NK):
                        ins = act.activation(hid_t[:, k, c, :, 0:NN],
                                             M2[:, c * GB * NN:(c + 1) * GB * NN].rearrange("p (b n) -> p b n", b=GB),
                                             ACT.Relu, bias=b1c[:, c, k:k + 1])
                    ins.then_inc(S["hid_t"], 1)
                elif kind == "l0_z" and k == 1:
                    wait(act, "z_mm", it, 2 * g + 2)
                    act.activation(z_s[:, NK - 1, :], M2[:, 0:P], ACT.Copy).then_inc(S["z_hi"], 1)
                elif kind == "l0_out":
                    wait(act, "o_mm", it, g + 1)
                    for c in range(NK):
                        ins = act.activation(o_r[:, c, :, :].rearrange("p b n -> p (b n)"), M2[:, c * GB * NN:(c + 1) * GB * NN],
                                             ACT.Relu, bias=fusion_b2[:, c:c + 1], scale=fusion[:, c:c + 1])
                    ins.then_inc(S["o_relu"], 1)
                elif kind == "adj_t":
                    wait(act, "adjt_mm", it, g + 1)
                    act.activation(cols(adjT[g]), M2[:, :], ACT.Copy).then_inc(S["adj_t"], 1)
                elif kind == "x1_t":
                    wait(act, "x1t_mm", it, g + 1)
                    act.activation(cols(xT[g]), M0[:, :], ACT.Copy).then_inc(S["x1_t"], 1)
                elif kind == "qkv":
                    wait(act, "k_mm", it, g + 1)
                    act.activation(cols(kT[g]), S0[:, :], ACT.Copy).then_inc(S["k_t"], 1)
                elif kind == "s":
                    wait(act, "s_neg", it, n + 1)
                    for h in range(HEADS):
                        S_ = S0 if h < GB else S1
                        ins = act.activation(e_s[:, h, :], S_[:, (h % GB) * P:(h % GB + 1) * P], ACT.Exp,
                                             bias=s_ng[:, h:h + 1], scale=SCALE)
                        if h % GB == GB - 1:
                            ins.then_inc(S["e_act"], 1)
                elif kind == "a" and k % 2:
                    wait(act, "av_mm", it, n + 1)
                    act.activation(o_ts[:, :, :, :].rearrange("p a h q -> p (a h q)"), M0[:, :], ACT.Copy).then_inc(S["o_t"], 1)
                elif kind == "on":
                    wait(act, "ont_mm", it, 2 * g + k + 1)
                    act.activation(on_ts[:, :, :].rearrange("p a q -> p (a q)"), M0[:, 0:2 * P], ACT.Copy).then_inc(S["on_t"], 1)
                elif kind == "x2_t":
                    wait(act, "x2t_mm", it, g + 1)
                    act.activation(cols(x2T[g]), M2[:, :], ACT.Copy).then_inc(S["x2_t"], 1)
                elif kind == "begin":
                    wait_g(act, "x3t_mm", g, it, 1)
                    act.activation(hT[g][:, :], RT[:, :], ACT.Copy).then_inc(SG["h_first"][g], 1)
                elif kind == "turn" and k:
                    wait_g(act, "h_mm", g, it, k)
                    act.activation(cols(h_tok[g]), RT[:, :], ACT.Copy).then_inc(SG["h_tok"][g], 1)
                elif kind == "r":
                    wait_g(act, "r_mm", g, it, k + 1)
                    act.activation(tr[g][:, :], RA[:, :], ACT.Tanh, bias=b_rz[:, 0:1], scale=0.5).then_inc(SG["r_act"][g], 1)
                elif kind == "hn":
                    wait_g(act, "hn_mm", g, it, k + 1)
                    act.activation(un[g][:, :], RB[:, :], ACT.Identity, bias=b_hn[:, 0:1]).then_inc(SG["u_act"][g], 1)
                elif kind == "z":
                    wait_g(act, "rw", g, it, k + 1)
                    act.activation(nn[g][:, :], tr[g][:, :], ACT.Tanh, bias=bih[:, 2:3]).then_inc(SG["n_act"][g], 1)
                    wait_g(act, "zg_mm", g, it, k + 1)
                    act.activation(tz[g][:, :], RB[:, :], ACT.Tanh, bias=b_rz[:, 1:2], scale=0.5).then_inc(SG["z_act"][g], 1)

            program(act, steps)

        @block.vector
        def _(dve):
            n = [0]

            def after(ins):
                n[0] += 1
                ins.then_inc(w_prep, 1)
                dve.wait_ge(w_prep, n[0])

            dve.wait_ge(w_in, 16 * WEIGHT_DMAS)
            after(dve.tensor_reduce(fw_s[:, 0:1], fw[:, :], AX_X, ALU.max))
            after(dve.tensor_scalar(fwx[:, :], fw[:, :], fw_s[:, 0:1], None, ALU.subtract))
            dve.wait_ge(w_exp, 1)
            after(dve.tensor_reduce(fw_s[:, 1:2], fw[:, :], AX_X, ALU.add))
            after(dve.reciprocal(fw_s[:, 2:3], fw_s[:, 1:2]))
            after(dve.tensor_scalar(fusion[:, :], fw[:, :], fw_s[:, 2:3], None, ALU.mult))
            dve.wait_ge(consts_ready, 1)
            after(dve.tensor_reduce(ident_small[:, :], ident[:, :].rearrange("p (b n) -> p n b", b=GB), AX_X, ALU.add))
            after(dve.tensor_tensor(member_x[:, :, :], member[:, :, :],
                                    ident_small[:, :].unsqueeze(1).broadcast_to([P, NK, NS]), ALU.mult))
            after(dve.tensor_reduce(member_p[:, :], member_x[:, :, :], AX_X, ALU.add))
            banks = [S0, S1, M0, M1, RT]
            for i in range(5):
                dve.wait_ge(w_mm, i + 1)
                m = min(4, 18 - 4 * i)
                dve.tensor_copy(wT[:, 4 * i:4 * i + m, :].rearrange("p a b -> p (a b)"), banks[i][:, 0:m * P]).then_inc(w_evac, 1)
            dve.wait_ge(w_evac, 5)
            after(dve.tensor_tensor(b_rz[:, :], bih, bhh, ALU.add))
            after(dve.tensor_scalar(b_rz[:, :], b_rz[:, :], 0.5, None, ALU.mult))
            after(dve.tensor_scalar(b_hn[:, :], bhh[:, 2:3], 0.5, None, ALU.mult))
            after(dve.tensor_tensor(fusion_b2[:, :], fusion[:, :], b2c, ALU.mult))
            dve.tensor_scalar(whn[:, :], wT[:, WHH + 2, :], 0.5, None, ALU.mult).then_inc(w_evac, 1)
            for i in range(LAYERS):
                dve.wait_ge(w_mm, 6 + i)
                ins = dve.tensor_copy(comp[:, i, :], [RA, RB, M2, S0, S1][i][:, 0:3 * P])
            ins.then_inc(w_evac, 1)

            def moments(at, y, st, m, v):
                for b in range(GB):
                    ins = dve.bn_stats(st[:, b, :], y[:, b, :])
                at(ins, 1)
                passed(dve)
                for b in range(GB):
                    ins = dve.bn_aggr(m[:, b, :], st[:, b, :])
                at(ins, 2)
                at(dve.tensor_scalar(v[:, :], m[:, :, 1], LN_EPS, None, ALU.add), 3)

            def front_norm(it, g, j, y):
                name = f"ln{j}"

                def at(ins, k):
                    ins.then_inc(S[name], 1)
                    if k < 3:
                        wait(dve, name, it, 3 * g + k)

                moments(at, y, stats[j - 1], mv[g][j - 1], ve[g][j - 1])

            def last_norm(it, g):
                def at(ins, k):
                    ins.then_inc(SG["ln4"][g], 1)
                    if k < 3:
                        wait_g(dve, "ln4", g, it, k)

                moments(at, y4[g], stats4[g], mv4[g], ve4[g])

            def normalise(o, y, m, r):
                for b in range(GB):
                    ins = dve.tensor_scalar(o[:, b, :], y[:, b, :], m[:, b, 0:1], r[:, b:b + 1], ALU.subtract, ALU.mult)
                return ins

            def steps(it, g, kind, k):
                n = GB * g + k
                if kind == "l0_prep":
                    done = [10 * g]

                    def then(ins):
                        done[0] += 1
                        ins.then_inc(S["l0_prep"], 1)
                        wait(dve, "l0_prep", it, done[0])

                    dve.wait_ge(small_in[g], (it + 1) * (16 * 2 * GB))
                    then(dve.tensor_tensor(a_i[:, :], adjc[g][:, :], ident_small[:, :], ALU.add))
                    then(dve.tensor_tensor(a_m[:, :, :], member[:, :, :], a_i[:, :].unsqueeze(1).broadcast_to([P, NK, NS]), ALU.mult))
                    then(dve.tensor_reduce(deg0[:, :], a_m[:, :, :], AX_X, ALU.add))
                    then(dve.tensor_scalar(deg0_z[:, :], deg0[:, :], 0.0, None, ALU.is_equal))
                    then(dve.tensor_tensor(deg0_s[:, :], deg0[:, :], deg0_z[:, :], ALU.add))
                    wait(dve, "l0_pow", it, g + 1)
                    then(dve.scalar_tensor_tensor(dinv0[:, :], deg0[:, :], 0.0, pow0[:, :], ALU.not_equal, ALU.mult))
                    then(dve.tensor_tensor(dinv0m[:, :], dinv0[:, :], member_p[:, :], ALU.mult))
                    then(dve.tensor_tensor(a_row[:, :, :], a_i[:, :].unsqueeze(1).broadcast_to([P, NK, NS]),
                                           dinv0m[:, :].unsqueeze(2).broadcast_to([P, NK, NS]), ALU.mult))
                    then(dve.transpose(a_col[:, :, :].rearrange("p k n -> p (k n)"), a_row[:, :, :].rearrange("p k n -> p (k n)")))
                    for q in range(GB):
                        r = slice(NS * q, NS * q + NS)
                        ins = dve.tensor_tensor(nat[r, :, q, :], a_col[r, :, 0:NN],
                                                dinv0m[r, :].unsqueeze(2).broadcast_to([NS, NK, NN]), ALU.mult)
                    then(ins)
                elif kind == "l0_z" and k == 0:
                    wait(dve, "z_mm", it, 2 * g + 1)
                    dve.tensor_copy(z_s[:, 0:GB, :].rearrange("p k d -> p (k d)"), M2[:, :]).then_inc(S["z_lo"], 1)
                elif kind == "l0_out":
                    wait(dve, "o_relu", it, g + 1)
                    dve.tensor_tensor(o_m[:, :, :, :], o_r[:, :, :, :],
                                      member[:, :, 0:NN].unsqueeze(2).broadcast_to([P, NK, GB, NN]), ALU.mult).then_inc(S["fused"], 1)
                    wait(dve, "fused", it, 2 * g + 1)
                    dve.tensor_reduce(f_t[:, :], o_m[:, :, :, :].rearrange("p k b n -> p (b n) k"), AX_X, ALU.add)\
                        .then_inc(S["fused"], 1)
                elif kind == "l0_add":
                    dve.wait_ge(x_in[g], (it + 1) * 16)
                    wait(dve, "fused_mm", it, g + 1)
                    dve.tensor_tensor(xin[g][0:NN, :, :].rearrange("p b d -> p (b d)"), M2[0:NN, :],
                                      xin[g][0:NN, :, :].rearrange("p b d -> p (b d)"), ALU.add).then_inc(S["y1"], 1)
                    wait(dve, "y1", it, g + 1)
                    front_norm(it, g, 1, xin[g])
                elif kind == "adj_t":
                    dve.wait_ge(adj_in[g], (it + 1) * 16)
                    dve.tensor_reduce(deg[g][:, :], adjn[g][:, :, :], AX_X, ALU.add).then_inc(S["deg"], 1)
                    wait(dve, "deg", it, 3 * g + 1)
                    dve.tensor_scalar(deg_z[g][:, :], deg[g][:, :], 0.0, None, ALU.is_equal).then_inc(S["deg"], 1)
                    wait(dve, "deg", it, 3 * g + 2)
                    dve.tensor_tensor(deg_s[g][:, :], deg[g][:, :], deg_z[g][:, :], ALU.add).then_inc(S["deg"], 1)
                elif kind == "x1":
                    wait(dve, "ln1_pow", it, g + 1)
                    normalise(x1[g], xin[g], mv[g][0], rs[g][0]).then_inc(S["x1"], 1)
                elif kind == "x2":
                    wait(dve, "ln2_pow", it, g + 1)
                    normalise(x2[g], y2[g], mv[g][1], rs[g][1]).then_inc(S["x2"], 1)
                    wait(dve, "deg_pow", it, g + 1)
                    dve.scalar_tensor_tensor(dinv[g][:, :], deg[g][:, :], 0.0, deg_p[g][:, :], ALU.not_equal, ALU.mult)\
                        .then_inc(S["dinv"], 1)
                elif kind == "qkv":
                    wait(dve, "q_mm", it, g + 1)
                    dve.tensor_copy(cols(qT[g]), S1[:, :]).then_inc(S["q_t"], 1)
                    wait(dve, "v_mm", it, g + 1)
                    dve.tensor_copy(vp[g][:, :, :, 0:DH], M1[:, :].rearrange("p (b h d) -> p b h d", b=GB, h=HEADS))\
                        .then_inc(S["v_p"], 1)
                elif kind == "s":
                    wait(dve, "s_mm", it, n + 1)
                    dve.tensor_reduce(s_mx[:, 0:GB], S0[:, :].rearrange("p (h k) -> p h k", h=GB), AX_X, ALU.max)
                    dve.tensor_reduce(s_mx[:, GB:HEADS], S1[:, :].rearrange("p (h k) -> p h k", h=GB), AX_X, ALU.max)\
                        .then_inc(S["s_max"], 1)
                    wait(dve, "s_max", it, n + 1)
                    dve.tensor_scalar(s_ng[:, :], s_mx[:, :], -SCALE, None, ALU.mult).then_inc(S["s_neg"], 1)
                elif kind == "t":
                    wait(dve, "adj_te", it, g + 1)
                    for j, S_ in enumerate((S0, S1)):
                        wait(dve, "et_mm", it, 2 * n + j + 1)
                        dve.tensor_tensor(p_s[:, GB * j:GB * j + GB, :], S_[:, :].rearrange("p (h q) -> p h q", h=GB),
                                          adjTe[g][:, k, :].unsqueeze(1).broadcast_to([P, GB, P]), ALU.mult).then_inc(S["p_t"], 1)
                elif kind == "u":
                    wait(dve, "u_mm", it, 2 * g + k + 1)
                    o4 = M1[:, :].rearrange("p (a h d) -> p a h d", a=2, h=HEADS)
                    dve.reciprocal(den[:, :, :], o4[:, :, :, DH]).then_inc(S["den"], 1)
                    wait(dve, "den", it, 2 * g + k + 1)
                    dve.tensor_tensor(o_ns[:, :, :, :], o4[:, :, :, 0:DH],
                                      den[:, :, :].unsqueeze(3).broadcast_to([P, 2, HEADS, DH]), ALU.mult).then_inc(S["o_n"], 1)
                elif kind == "wo":
                    wait(dve, "x1_b", it, g + 1)
                    wait(dve, "wo_mm", it, 2 * g + k + 1)
                    dve.tensor_tensor(y2[g][:, 2 * k:2 * k + 2, :].rearrange("p a d -> p (a d)"), M1[:, 0:2 * P],
                                      x1b[g][:, 2 * k:2 * k + 2, :].rearrange("p a d -> p (a d)"), ALU.add).then_inc(S["y2"], 1)
                    if k == 1:
                        wait(dve, "y2", it, 2 * g + 2)
                        front_norm(it, g, 2, y2[g])
                elif kind == "l2_t":
                    wait(dve, "t_mm", it, g + 1)
                    dve.tensor_tensor(t_b[:, :, :], M2[:, :].rearrange("p (b d) -> p b d", b=GB),
                                      l2b_row[:, :].unsqueeze(1).broadcast_to([P, GB, P]), ALU.add).then_inc(S["t_b"], 1)
                elif kind == "l2_agg":
                    wait(dve, "a_mm", it, g + 1)
                    wait(dve, "x2", it, g + 1)
                    dve.scalar_tensor_tensor(a_r[:, :, :], M2[:, :].rearrange("p (b d) -> p b d", b=GB), 0.0,
                                             per_graph(dinv[g][:, :]), ALU.max, ALU.mult).then_inc(S["a_relu"], 1)
                    wait(dve, "a_relu", it, g + 1)
                    dve.tensor_tensor(cols(y3[g]), cols(a_r), cols(x2[g]), ALU.add).then_inc(S["y3"], 1)
                    wait(dve, "y3", it, g + 1)
                    front_norm(it, g, 3, y3[g])
                elif kind == "bin":
                    dve.wait_ge(adjr_in[g], (it + 1) * 16)
                    dve.tensor_scalar(cols(a_bin[g]), cols(adjr[g]), 0.0, None, ALU.not_equal).then_inc(SG["a_bin"][g], 1)
                elif kind == "x3":
                    wait(dve, "ln3_pow", it, g + 1)
                    normalise(x3[g], y3[g], mv[g][2], rs[g][2]).then_inc(SG["x3"][g], 1)
                elif kind == "agg":
                    wait_g(dve, "agg_mm", g, it, k + 1)
                    dve.tensor_copy(agg[g][:, :], RT[:, :]).then_inc(SG["agg_t"][g], 1)
                elif kind == "hn":
                    wait_g(dve, "r_act", g, it, k + 1)
                    wait_g(dve, "u_act", g, it, k + 1)
                    dve.scalar_tensor_tensor(un[g][:, :], tr[g][:, :], 1.0, un[g][:, :], ALU.add, ALU.mult).then_inc(SG["rv"][g], 1)
                elif kind == "in":
                    wait_g(dve, "rv", g, it, k + 1)
                    wait_g(dve, "in_mm", g, it, k + 1)
                    dve.tensor_tensor(tr[g][:, :], RA[:, :], un[g][:, :], ALU.add).then_inc(SG["rw"][g], 1)
                elif kind == "z":
                    wait_g(dve, "hd", g, it, k + 1)
                    wait_g(dve, "z_act", g, it, k + 1)
                    dve.scalar_tensor_tensor(hd[g][:, :], tz[g][:, :], 1.0, hd[g][:, :], ALU.add, ALU.mult).then_inc(SG["he"][g], 1)
                    wait_g(dve, "he", g, it, k + 1)
                    dve.scalar_tensor_tensor(hT[g][:, :], hd[g][:, :], 0.5, nn[g][:, :], ALU.mult, ALU.add).then_inc(SG["h_new"][g], 1)
                elif kind == "end":
                    wait_g(dve, "f_mm", g, it, 1)
                    for b in range(GB):
                        in_graph = wT[:, MASK, bass.ds(it * (NG * GB) + g * GB + b, 1)]
                        ins = dve.scalar_tensor_tensor(y4[g][:, b, :], RT[:, b * P:(b + 1) * P], in_graph,
                                                       x3[g][:, b, :], ALU.mult, ALU.add)
                    ins.then_inc(SG["y4"][g], 1)
                    wait_g(dve, "y4", g, it, 1)
                    last_norm(it, g)
                    wait_g(dve, "ln4_pow", g, it, 1)
                    dve.wait_ge(out_done[g], (it + 1) * 16)
                    normalise(x4[g], y4[g], mv4[g], rs4[g]).then_inc(SG["x4"][g], 1)

            program(dve, steps)

        @block.tensor
        def _(pe):
            def turn(o, i, rows=P):
                return pe.transpose(o, i, ident[0:rows, 0:rows])

            pe.wait_ge(consts_ready, 1)
            pe.wait_ge(w_in, 16 * WEIGHT_DMAS)
            banks = [S0, S1, M0, M1, RT]
            for i in range(18):
                ins = turn(banks[i // 4][:, (i % 4) * P:(i % 4 + 1) * P], stage[:, i, :])
                if i % 4 == 3 or i == 17:
                    ins.then_inc(w_mm, 1)
            pe.wait_ge(w_evac, 5)
            for i in range(LAYERS):
                pe.matmul([RA, RB, M2, S0, S1][i][:, 0:3 * P], wT[:, WL + i, :], wT[:, WIH:WIH + 3, :].rearrange("p c f -> p (c f)"),
                          start=True, stop=True).then_inc(w_mm, 1)
            pe.wait_ge(w_evac, 7)

            def gate(o, l, c, w, g, last):
                if c is not None:
                    ins = pe.matmul(o[:, :], comp[:, l, c * P:(c + 1) * P], agg[g][:, :], start=True, stop=w is None)
                if w is not None:
                    ins = pe.matmul(o[:, :], w, hT[g][:, :], start=c is None, stop=True)
                ins.then_inc(SG[last][g], 1)

            def slot_before(name, it, g, k):
                g2, k2 = BEFORE[g, k]
                back = LAG_OF[g2, k2] - LAG_OF[g, k] + (SLOTS.index((g, k)) == 0)
                if not (isinstance(it, int) and not 0 <= it - back < ITERS):
                    wait_g(pe, name, g2, it - back, k2 + 1)

            def steps(it, g, kind, k):
                n = GB * g + k
                if kind == "l0_y":
                    wait(pe, "l0_prep", it, 10 * g + 10)
                    pe.wait_ge(small_in[g], (it + 1) * (16 * 2 * GB))
                    if not (isinstance(it, int) and it + g == 0):
                        wait(pe, "y1", it + g - 1, 2 - g)
                    pe.matmul(M2[:, 0:NK * GB * NN], xs[g][:, :], nat[:, :, :, :].rearrange("p k b n -> p (k b n)"),
                              start=True, stop=True).then_inc(S["y_mm"], 1)
                elif kind == "l0_hid":
                    if k == 0:
                        wait(pe, "y_t", it, g + 1)
                    else:
                        wait(pe, "hid_t", it, 2 * g + 1)
                    for c in range(NK):
                        ins = pe.matmul(M2[:, c * GB * NN:(c + 1) * GB * NN], W1s[:, c, k * P:(k + 1) * P],
                                        y_t[:, c, :, :].rearrange("p b n -> p (b n)"), start=True, stop=True)
                    ins.then_inc(S["w1_mm"], 1)
                elif kind == "l0_z":
                    if k == 0:
                        wait(pe, "hid_t", it, 2 * g + 2)
                    else:
                        wait(pe, "z_lo", it, g + 1)
                    for c in (range(GB) if k == 0 else [NK - 1]):
                        for h in range(2):
                            ins = pe.matmul(M2[:, (c % GB) * P:(c % GB + 1) * P], hid_t[:, h, c, :, :].rearrange("p b n -> p (b n)"),
                                            W2s[:, c, h, :], start=(h == 0), stop=(h == 1))
                    ins.then_inc(S["z_mm"], 1)
                elif kind == "l0_out":
                    wait(pe, "z_hi", it, g + 1)
                    for c in range(NK):
                        ins = pe.matmul(M2[:, c * GB * NN:(c + 1) * GB * NN], z_s[:, c, :],
                                        nat[:, c, :, :].rearrange("p b n -> p (b n)"), start=True, stop=True)
                    ins.then_inc(S["o_mm"], 1)
                elif kind == "adj_t":
                    pe.wait_ge(adj_in[g], (it + 1) * 16)
                    if isinstance(it, int) and it == 0:
                        wait(pe, "o_relu", it, g + 1)
                    else:
                        wait(pe, "a_relu", it - 1, g + 1)
                    for q in range(GB):
                        ins = turn(M2[:, q * P:(q + 1) * P], adjn[g][:, q, :])
                    ins.then_inc(S["adjt_mm"], 1)
                elif kind == "l0_add":
                    wait(pe, "fused", it, 2 * g + 2)
                    wait(pe, "adj_t", it, g + 1)
                    for q in range(GB):
                        ins = pe.matmul(M2[0:NN, q * P:(q + 1) * P], f_t[:, q * NN:(q + 1) * NN], ident[:, :], start=True, stop=True)
                    ins.then_inc(S["fused_mm"], 1)
                elif kind == "x1_t":
                    wait(pe, "x1", it, g + 1)
                    for q in range(GB):
                        ins = turn(M0[:, q * P:(q + 1) * P], x1[g][:, q, :])
                    ins.then_inc(S["x1t_mm"], 1)
                elif kind == "qkv":
                    wait(pe, "x1_t", it, g + 1)
                    pe.matmul(S0[:, :], wT[:, WK, :], cols(xT[g]), start=True, stop=True).then_inc(S["k_mm"], 1)
                    pe.matmul(S1[:, :], wT[:, WQ, :], cols(xT[g]), start=True, stop=True).then_inc(S["q_mm"], 1)
                    for q in range(GB):
                        ins = pe.matmul(M1[:, q * P:(q + 1) * P], xT[g][:, q, :], wT[:, WV, :], start=True, stop=True)
                    ins.then_inc(S["v_mm"], 1)
                elif kind == "s":
                    if k == 0:
                        wait(pe, "k_t", it, g + 1)
                        wait(pe, "q_t", it, g + 1)
                        pe.wait_ge(km_in[g], (it + 1) * (16 * HEADS))
                    else:
                        wait(pe, "p_t", it, 2 * n)
                    for j, S_ in enumerate((S0, S1)):
                        ins = pe.matmul(S_[:, :], qT[g][:, k, :], km[g][:, k, GB * j:GB * j + GB, :].rearrange("p h k -> p (h k)"),
                                        start=True, stop=True)
                    ins.then_inc(S["s_mm"], 1)
                elif kind == "t":
                    for j, S_ in enumerate((S0, S1)):
                        wait(pe, "e_act", it, 2 * n + j + 1)
                        for h in range(GB):
                            ins = turn(S_[:, h * P:(h + 1) * P], e_s[:, GB * j + h, :])
                        ins.then_inc(S["et_mm"], 1)
                elif kind == "a":
                    if k == 0:
                        wait(pe, "v_p", it, g + 1)
                    if k == 2:
                        wait(pe, "on_t", it, 2 * g + 1)
                    for h in range(HEADS):
                        wait(pe, "p_t", it, 2 * n + h // GB + 1) if h % GB == 0 else None
                        c = (k % 2) * 2 * P + (h // GB) * P
                        r = NS * (h % GB)
                        ins = pe.matmul(M0[r:r + NS, c:c + P], vp[g][:, k, h, :], p_s[:, h, :], start=True, stop=True)
                    ins.then_inc(S["av_mm"], 1)
                elif kind == "u":
                    wait(pe, "o_t", it, 2 * g + k + 1)
                    if k == 0:
                        wait(pe, "v_p", it, g + 1)
                    else:
                        wait(pe, "y2", it, 2 * g + 1)
                    for j in range(4):
                        ins = turn(M1[:, j * P:(j + 1) * P], o_ts[:, j // 2, j % 2, :])
                    ins.then_inc(S["u_mm"], 1)
                elif kind == "on":
                    wait(pe, "o_n", it, 2 * g + k + 1)
                    for j in range(2):
                        ins = turn(M0[:, j * P:(j + 1) * P], o_ns[:, j, :, :].rearrange("p h d -> p (h d)"))
                    ins.then_inc(S["ont_mm"], 1)
                elif kind == "wo":
                    wait(pe, "on_t", it, 2 * g + k + 1)
                    for j in range(2):
                        ins = pe.matmul(M1[:, j * P:(j + 1) * P], on_ts[:, j, :], wT[:, WO, :], start=True, stop=True)
                    ins.then_inc(S["wo_mm"], 1)
                elif kind == "x2_t":
                    wait(pe, "x2", it, g + 1)
                    if not (isinstance(it, int) and it + 1 == ITERS):
                        wait(pe, "o_relu", it + 1, g + 1)
                    for q in range(GB):
                        ins = turn(M2[:, q * P:(q + 1) * P], x2[g][:, q, :])
                    ins.then_inc(S["x2t_mm"], 1)
                elif kind == "l2_t":
                    wait(pe, "x2_t", it, g + 1)
                    for q in range(GB):
                        ins = pe.matmul(M2[:, q * P:(q + 1) * P], x2T[g][:, q, :], wT[:, WL2, :], start=True, stop=True)
                    ins.then_inc(S["t_mm"], 1)
                elif kind == "l2_agg":
                    wait(pe, "t_d", it, g + 1)
                    for q in range(GB):
                        ins = pe.matmul(M2[:, q * P:(q + 1) * P], adjT[g][:, q, :], t_d[:, q, :], start=True, stop=True)
                    ins.then_inc(S["a_mm"], 1)
                elif kind == "begin":
                    wait_g(pe, "x3", g, it, 1)
                    if not (isinstance(it, int) and it + g == 0):
                        wait_g(pe, "agg_t", 1 - g, it + g - 1, 3)
                    for q in range(GB):
                        ins = turn(RT[:, q * P:(q + 1) * P], x3[g][:, q, :])
                    ins.then_inc(SG["x3t_mm"][g], 1)
                elif kind == "turn" and k:
                    wait_g(pe, "h_new", g, it, k)
                    slot_before("agg_t", it, g, k)
                    if k == 2 and not (isinstance(it, int) and it + g == 0):
                        wait_g(pe, "y4", 1 - g, it + g - 1, 1)
                    for q in range(GB):
                        ins = turn(RT[:, q * P:(q + 1) * P], hT[g][:, q * P:(q + 1) * P])
                    ins.then_inc(SG["h_mm"][g], 1)
                elif kind == "agg":
                    if k == 0:
                        wait_g(pe, "a_bin", g, it, 1)
                        wait_g(pe, "h_first", g, it, 1)
                    else:
                        wait_g(pe, "h_tok", g, it, k)
                    src = x3[g] if k == 0 else h_tok[g]
                    for q in range(GB):
                        ins = pe.matmul(RT[:, q * P:(q + 1) * P], src[:, q, :], a_bin[g][:, q, :], start=True, stop=True)
                    ins.then_inc(SG["agg_mm"][g], 1)
                elif kind == "r":
                    wait_g(pe, "agg_t", g, it, k + 1)
                    slot_before("rw", it, g, k)
                    gate(RA, k, 0, wT[:, WHH, :], g, "r_mm")
                elif kind == "hn":
                    slot_before("z_act", it, g, k)
                    gate(RB, k, None, whn[:, :], g, "hn_mm")
                elif kind == "in":
                    wait_g(pe, "r_act", g, it, k + 1)
                    gate(RA, k, 2, None, g, "in_mm")
                elif kind == "z":
                    wait_g(pe, "u_act", g, it, k + 1)
                    gate(RB, k, 1, wT[:, WHH + 1, :], g, "zg_mm")
                elif kind == "end":
                    wait_g(pe, "h_new", g, it, LAYERS)
                    for q in range(GB):
                        ins = turn(RT[:, q * P:(q + 1) * P], hT[g][:, q * P:(q + 1) * P])
                    ins.then_inc(SG["f_mm"][g], 1)

            program(pe, steps)


_INS = ['x', 'adj', 'nodemask', 'L0_gnn_W1', 'L0_gnn_b1', 'L0_gnn_W2', 'L0_gnn_b2', 'L0_gnn_fusion_w', 'L1_gnn_Wq',
        'L1_gnn_Wk', 'L1_gnn_Wv', 'L1_gnn_Wo', 'L1_gnn_bo', 'L2_gnn_W', 'L2_gnn_b', 'L3_gnn_weight', 'L3_gnn_w_ih',
        'L3_gnn_w_hh', 'L3_gnn_b_ih', 'L3_gnn_b_hh']


def kernel(**inputs):
    import numpy as _np
    import concourse.bacc as _bacc
    from concourse import mybir as _mybir
    from concourse.bass_utils import run_bass_kernel_spmd as _run

    nc = _bacc.Bacc("TRN2", target_bir_lowering=False, num_devices=1)
    arrays, args = {}, []
    for name in _INS:
        a = _np.ascontiguousarray(inputs[name])
        arrays[f"in_{name}_dram"] = a
        args.append(nc.dram_tensor(f"in_{name}_dram", a.shape, _mybir.dt.from_np(a.dtype), kind="ExternalInput").ap())
    args.append(nc.dram_tensor("out_0_dram", inputs["x"].shape, _mybir.dt.float32, kind="ExternalOutput").ap())
    gnn_stack_kernel(nc, *args)
    r = _run(nc, [arrays], core_ids=[0])
    return r.results[0]["out_0_dram"]
```

```python
from contextlib import ExitStack

import concourse.bass as bass
from concourse import mybir

F32 = mybir.dt.float32
F32R = mybir.dt.float32r
ALU = mybir.AluOpType
ACT = mybir.ActivationFunctionType
AX_X = mybir.AxisListType.X

P = 128
GB = 4
NG = 2
W = GB * P
HEADS, DH = 8, 16
NN, NS = 25, 32
GROUPS = [list(range(25)), [0, 1, 2, 3, 4, 5, 6, 7, 8], [0, 9, 10, 11, 12, 13, 14],
          [6, 7, 8, 12, 13, 14], [3, 4, 5, 9, 10, 11]]
NK = len(GROUPS)
LAYERS = 5
LN_EPS, ADJ_EPS = 1e-5, 1e-6
SCALE = float(DH) ** -0.5

PER = dict(
    l0_prep=10 * NG, l0_pow=NG, y_mm=NG, y_t=NG, w1_mm=2 * NG, hid_t=2 * NG, z_mm=2 * NG, z_lo=NG, z_hi=NG,
    o_mm=NG, o_relu=NG, fused=2 * NG, fused_mm=NG, y1=NG,
    ln1=3 * NG, ln1_pow=NG, ln2=3 * NG, ln2_pow=NG, ln3=3 * NG, ln3_pow=NG, x1=NG, x2=NG,
    adjt_mm=NG, adj_t=NG, adj_te=NG, x1t_mm=NG, x1_t=NG, x1_b=NG, k_mm=NG, q_mm=NG, v_mm=NG, k_t=NG, q_t=NG, v_p=NG,
    s_mm=GB * NG, s_max=GB * NG, s_neg=GB * NG, e_act=2 * GB * NG, et_mm=2 * GB * NG, p_t=2 * GB * NG,
    av_mm=GB * NG, o_t=2 * NG, u_mm=2 * NG, den=2 * NG, o_n=2 * NG, ont_mm=2 * NG, on_t=2 * NG, wo_mm=2 * NG, y2=2 * NG,
    deg=3 * NG, deg_pow=NG, dinv=NG, x2t_mm=NG, x2_t=NG, t_mm=NG, t_b=NG, t_d=NG, a_mm=NG, a_relu=NG, y3=NG,
)
PER_GRU = dict(
    a_bin=1, x3=1, x3t_mm=1, h_first=1, h_mm=LAYERS - 1, h_tok=LAYERS - 1,
    agg_mm=LAYERS, agg_t=LAYERS, r_mm=LAYERS, hn_mm=LAYERS, in_mm=LAYERS, zg_mm=LAYERS,
    r_act=LAYERS, u_act=LAYERS, n_act=LAYERS, z_act=LAYERS, rv=LAYERS, rw=LAYERS, h_hi=LAYERS, h_lo=LAYERS, agg_hi=LAYERS, hd=LAYERS, he=LAYERS, h_new=LAYERS,
    f_mm=1, y4=1, ln4=3, ln4_pow=1, x4=1,
)
LAG = 3


MERGE = dict(
    tensor="AABRBRABRBRRBRBRAARRRRRBARARARRABARRBAARARAARRABRRRAAARRABRRRAARRABBRRRRABARRRRABARBARARR",
    vector="BRRBABAABRBRARRRRRRABRABARRRAARRARBAARBRRRAAAARBARBRRRRARRAAARABRARABRRRBARRRRAARRARRRABB",
    scalar="AABBARRBBRRRBABRRRRAAARBARBRARRRABRRAAAARRRARARRABRRBAARRRARBRRRAARABRRAARBABRRAARBRRRRRA",
    gpsimd="BARRBBARRRBRRAAAAARRBBRAAARBRAARRARRRRRRBARAABRAARRRBBRRARARRRABARRRRRAARRARAABRRBRBRRAAB",
)


def attention_steps(half):
    at = (1, half)
    out = [(*at, "te", 0), (*at, "x1_t", 0), (*at, "qkv", 0)]
    for b in range(GB):
        out += [(*at, "s", b), (*at, "max", b), (*at, "t", b), (*at, "p", b)]
        if b == 2:
            out += [(*at, "on", 0), (*at, "wo", 0)]
        out += [(*at, "a", b)]
        if b == 1:
            out += [(*at, "u", 0)]
    return out + [(*at, "u", 1), (*at, "on", 1), (*at, "wo", 1)]


def first_third_steps(half):
    end, last, start = (1 - half, 1 - half), (2 - half, 1 - half), (0, half)
    return [(*end, "l0_z", 0), (*end, "l0_z", 1), (*end, "l0_out", 0),
            (*last, "x2", 0), (*end, "l0_fuse", 0), (*last, "x2_t", 0), (*last, "l2_t", 0), (*last, "l2_agg", 0),
            (*end, "adj_t", 0), (*end, "l0_add", 0),
            (*start, "l0_deg", 0), (*end, "x1", 0), (*start, "l0_prep", 0), (*start, "l0_y", 0), (*start, "l0_hid", 0), (*start, "l0_hid", 1)]


def gated_steps(half):
    this, other, new = (2, half), (3 - half, 1 - half), (2 - half, 1 - half)
    slots = [(*this, 0), (*other, 3), (*this, 1), (*other, 4), (*this, 2)]
    out = []
    for n, (lag, g, layer) in enumerate(slots):
        def step(kind):
            return lag, g, kind, layer

        if n == 0:
            out += [step("agg"), step("agg_lo")]
        out += [step("r")]
        if n:
            before = slots[n - 1]
            out += [(*before[:2], "h_new", before[2])]
        out += [step("hn")]
        if n + 1 < len(slots):
            nxt = slots[n + 1]
            out += [(*nxt[:2], "turn", nxt[2]), step("in"), (*nxt[:2], "agg", nxt[2]), (*nxt[:2], "agg_lo", nxt[2]), step("z")]
        else:
            out += [step("in"), (*other, "end", 0), (*new, "bin", 0), (*new, "x3", 0), step("z"),
                    (*new, "begin", 0), (*other, "out", 0), step("h_new")]
    return out


def body_steps(merge):
    out = []
    for half in range(NG):
        threads = dict(A=iter(attention_steps(half)), B=iter(first_third_steps(half)), R=iter(gated_steps(half)))
        out += [(thread, *next(threads[thread])) for thread in merge]
    return out


BODY = {engine: body_steps(merge) for engine, merge in MERGE.items()}
SLOTS = [(g, k) for thread, _, g, kind, k in BODY["tensor"] if kind == "agg"]
BEFORE = {slot: SLOTS[n - 1] for n, slot in enumerate(SLOTS)}
LAG_OF = {(g, k): lag for thread, lag, g, kind, k in BODY["tensor"] if kind == "agg"}


def gnn_stack_kernel(nc, x, adj, nodemask, W1, b1, W2, b2, fusion_w, Wq, Wk, Wv, Wo, bo, L2W, L2b,
                     Wl, w_ih, w_hh, b_ih, b_hh, out):
    NB = x.shape[0]
    ITERS = NB // (GB * NG)
    with ExitStack() as ctx:
        def sb(name, shape, dt=F32):
            return ctx.enter_context(nc.sbuf_tensor(name, shape, dt))

        def sem(name):
            return ctx.enter_context(nc.semaphore(name))

        S = {name: sem(name) for name in PER}
        SG = {name: [sem(f"{name}_g{g}") for g in range(NG)] for name in PER_GRU}
        consts_ready, w_in, w_prep, w_mm, w_evac = (sem(n) for n in ("consts_ready", "w_in", "w_prep", "w_mm", "w_evac"))
        wait_over = sem("wait_over")
        w_exp, w_pool = sem("w_exp"), sem("w_pool")
        x_in = [sem(f"x_in{g}") for g in range(NG)]
        small_in = [sem(f"small_in{g}") for g in range(NG)]
        adj_in = [sem(f"adj_in{g}") for g in range(NG)]
        adjr_in = [sem(f"adjr_in{g}") for g in range(NG)]
        km_in = [sem(f"km_in{g}") for g in range(NG)]
        out_done = [sem(f"out_done{g}") for g in range(NG)]

        def wait(eng, name, it, k):
            eng.wait_ge(S[name], it * PER[name] + k)

        def wait_g(eng, name, g, it, k):
            eng.wait_ge(SG[name][g], it * PER_GRU[name] + k)

        def wait_before(eng, name, it, g):
            if not (isinstance(it, int) and it + g == 0):
                wait(eng, name, it + g - 1, PER[name] // NG * (NG - g))

        def passed(eng):
            eng.sem_inc(wait_over, 1)

        def program(eng, engine, steps):
            def iteration(it, some):
                for thread, lag, g, kind, k in BODY[engine]:
                    if not some or 0 <= it - lag < ITERS:
                        steps(it - lag, g, kind, k)

            for it in range(LAG):
                iteration(it, True)
            with eng.Fori(LAG, ITERS) as it:
                iteration(it, False)
            for it in range(ITERS, ITERS + LAG):
                iteration(it, True)

        ident = sb("ident", [P, P])
        ident_small = sb("ident_small", [P, NS])
        member = sb("member", [P, NK, NS])
        member_p = sb("member_p", [P, NK])
        member_x = sb("member_x", [P, NK, NS])
        half_neg = sb("half_neg", [P, NK])
        stage = sb("stage", [P, 18, P])
        wT = sb("wT", [P, 18, P])
        WQ, WK, WV, WO, WL2, WHH, WIH, WL, MASK, BIAS = 0, 1, 2, 3, 4, 5, 8, 11, 16, 17
        comp_hi = sb("comp_hi", [P, LAYERS, 3 * P], F32R)
        comp_lo = sb("comp_lo", [P, LAYERS, 3 * P], F32R)
        whh_hi = sb("whh_hi", [P, 3, P], F32R)
        whh_lo = sb("whh_lo", [P, 3, P], F32R)
        W1s = sb("W1s", [P, NK, 2 * P])
        W2s = sb("W2s", [P, NK, 2, P])
        b1c = wT[:, BIAS, 0:2 * NK].rearrange("p (g h) -> p g h", h=2)
        b2c = wT[:, BIAS, 2 * NK:3 * NK]
        fw = sb("fw", [P, NK])
        fwx = sb("fwx", [P, NK])
        fw_s = sb("fw_s", [P, 4])
        fusion = sb("fusion", [P, NK])
        fusion_b2 = sb("fusion_b2", [P, NK])
        bih = wT[:, BIAS, 15:18]
        bhh = wT[:, BIAS, 18:21]
        b_rz = sb("b_rz", [P, 3])
        b_hn = sb("b_hn", [P, 1])
        bo_row = sb("bo_row", [P, P])
        l2b_row = sb("l2b_row", [P, P])

        xin = [sb(f"xin_{g}", [P, GB, P]) for g in range(NG)]
        xs = [sb(f"xs_{g}", [P, P]) for g in range(NG)]
        adjc = [sb(f"adjc_{g}", [P, NS]) for g in range(NG)]
        adjn = [sb("adjn", [P, GB, P])] * NG
        adjr = [sb(f"adjr_{g}", [P, GB, P]) for g in range(NG)]
        a_i = sb("a_i", [P, NS])
        a_m = sb("a_m", [P, NK, NS])
        deg0 = sb("deg0", [P, NK])
        deg0_z = sb("deg0_z", [P, NK])
        deg0_s = sb("deg0_s", [P, NK])
        pow0 = sb("pow0", [P, NK])
        dinv0 = sb("dinv0", [P, NK])
        dinv0m = sb("dinv0m", [P, NK])
        a_row = sb("a_row", [P, NK, NS])
        a_col = sb("a_col", [P, NK, NS])
        nat = sb("nat", [P, NK, GB, NN])
        y_t = sb("y_t", [P, NK, GB, NN])
        hid_t = sb("hid_t", [P, 2, NK, GB, NS])
        z_s = sb("z_s", [P, NK, P])
        o_r = sb("o_r", [P, NK, GB, NN])
        o_m = sb("o_m", [P, NK, GB, NN])
        f_t = sb("f_t", [P, GB * NN])
        stats = [sb(f"stats_{j}", [P, GB, 6]) for j in range(3)]
        mv = [[sb(f"mv_{g}{j}", [P, GB, 2]) for j in range(3)] for g in range(NG)]
        ve = [[sb(f"ve_{g}{j}", [P, GB]) for j in range(3)] for g in range(NG)]
        rs = [[sb(f"rs_{g}{j}", [P, GB]) for j in range(3)] for g in range(NG)]
        x1 = [sb("x1", [P, GB, P])] * NG
        x1b = [sb("x1b", [P, GB, P])] * NG
        x2 = [sb("x2", [P, GB, P])] * NG
        y2 = [sb(f"y2_{g}", [P, GB, P]) for g in range(NG)]
        y3 = [sb(f"y3_{g}", [P, GB, P]) for g in range(NG)]
        adjT = [sb(f"adjT_{g}", [P, GB, P]) for g in range(NG)]
        adjTe = [sb("adjTe", [P, GB, P])] * NG
        xT = [sb("xT", [P, GB, P])] * NG
        x2T = [sb("x2T", [P, GB, P])] * NG
        kT = [sb("kT", [P, GB, P])] * NG
        qT = [sb("qT", [P, GB, P])] * NG
        km = [sb("km", [P, GB, HEADS, P])] * NG
        vp = [sb("vp", [P, GB, HEADS, NS])] * NG
        s_mx = sb("s_mx", [P, HEADS])
        s_ng = sb("s_ng", [P, HEADS])
        e_s = sb("e_s", [P, HEADS, P])
        p_s = sb("p_s", [P, HEADS, P])
        o_ts = sb("o_ts", [P, 2, 2, P])
        den = sb("den", [P, 2, HEADS])
        o_ns = sb("o_ns", [P, 2, HEADS, DH])
        on_ts = sb("on_ts", [P, 2, P])
        deg = [sb(f"deg_{g}", [P, GB]) for g in range(NG)]
        deg_z = [sb(f"deg_z_{g}", [P, GB]) for g in range(NG)]
        deg_s = [sb(f"deg_s_{g}", [P, GB]) for g in range(NG)]
        deg_p = [sb(f"deg_p_{g}", [P, GB]) for g in range(NG)]
        dinv = [sb(f"dinv_{g}", [P, GB]) for g in range(NG)]
        t_b = sb("t_b", [P, GB, P])
        t_d = sb("t_d", [P, GB, P])
        a_r = sb("a_r", [P, GB, P])

        x3 = [sb(f"x3_{g}", [P, GB, P]) for g in range(NG)]
        a_bin = [sb(f"a_bin_{g}", [P, GB, P]) for g in range(NG)]
        hT = [sb(f"hT_{g}", [P, W]) for g in range(NG)]
        h_tok = [sb(f"h_tok_{g}", [P, GB, P]) for g in range(NG)]
        h_hi = [sb(f"h_hi_{g}", [P, W], F32R) for g in range(NG)]
        h_lo = [sb(f"h_lo_{g}", [P, W], F32R) for g in range(NG)]
        agg_hi = [sb(f"agg_hi_{g}", [P, W], F32R) for g in range(NG)]
        agg_lo = [sb(f"agg_lo_{g}", [P, W], F32R) for g in range(NG)]
        tr = [sb(f"tr_{g}", [P, W]) for g in range(NG)]
        tz = [sb(f"tz_{g}", [P, W]) for g in range(NG)]
        un = [sb(f"un_{g}", [P, W]) for g in range(NG)]
        nn = [sb(f"nn_{g}", [P, W]) for g in range(NG)]
        hd = [sb(f"hd_{g}", [P, W]) for g in range(NG)]
        y4 = [sb(f"y4_{g}", [P, GB, P]) for g in range(NG)]
        x4 = [sb(f"x4_{g}", [P, GB, P]) for g in range(NG)]
        stats4 = [sb(f"stats4_{g}", [P, GB, 6]) for g in range(NG)]
        mv4 = [sb(f"mv4_{g}", [P, GB, 2]) for g in range(NG)]
        ve4 = [sb(f"ve4_{g}", [P, GB]) for g in range(NG)]
        rs4 = [sb(f"rs4_{g}", [P, GB]) for g in range(NG)]

        def bank(name):
            return ctx.enter_context(nc.psum_tensor(name, [P, 512], F32))

        S0, S1, M0, M1, M2, RT, RA, RB = (bank(n) for n in ("S0", "S1", "M0", "M1", "M2", "RT", "RA", "RB"))

        def cols(t):
            return t[:, :, :].rearrange("p b d -> p (b d)")

        def per_graph(v):
            return v.unsqueeze(2).broadcast_to([P, GB, P])

        xr = x.rearrange("b n d -> n b d")
        ar = adj.rearrange("b n m -> n b m")
        outr = out.rearrange("b n d -> n b d")
        WEIGHT_DMAS = 5 + 1 + 1 + 1 + 1 + 1 + 2 + 4 + 2 + 1
        block = ctx.enter_context(nc.Block())

        @block.sync
        def _(sp):
            for i, w in enumerate((Wq, Wk, Wv, Wo, L2W)):
                sp.dma_start(stage[:, i, :], w).then_inc(w_in, 16)
            sp.dma_start(stage[:, WHH:WHH + 3, :], w_hh.rearrange("(c p) d -> p c d", p=P)).then_inc(w_in, 16)
            sp.dma_start(stage[:, WIH:WIH + 3, :], w_ih.rearrange("(c p) d -> p c d", p=P)).then_inc(w_in, 16)
            sp.dma_start(stage[:, WL:WL + LAYERS, :], Wl.rearrange("l c d -> c l d")).then_inc(w_in, 16)
            sp.dma_start(stage[:, MASK, :], nodemask).then_inc(w_in, 16)
            sp.dma_start(W1s[:, :, :], W1.rearrange("g d e -> d g e")).then_inc(w_in, 16)
            for h in range(2):
                sp.dma_start(W2s[:, :, h, :], W2[:, h * P:(h + 1) * P, :].rearrange("g e d -> e g d")).then_inc(w_in, 16)
            sp.wait_ge(w_pool, 1)
            sp.dma_start(stage[0:10, BIAS, :], b1.rearrange("g (h p) -> (g h) p", p=P)).then_inc(w_in, 16)
            sp.dma_start(stage[10:15, BIAS, :], b2).then_inc(w_in, 16)
            sp.dma_start(stage[15:18, BIAS, :], b_ih.rearrange("(c p) -> c p", p=P)).then_inc(w_in, 16)
            sp.dma_start(stage[18:21, BIAS, :], b_hh.rearrange("(c p) -> c p", p=P)).then_inc(w_in, 16)
            sp.dma_start(bo_row[:, :], bo.partition_broadcast(P)).then_inc(w_in, 16)
            sp.dma_start(l2b_row[:, :], L2b.partition_broadcast(P)).then_inc(w_in, 16)
            sp.dma_start(fw[:, :], fusion_w.partition_broadcast(P)).then_inc(w_in, 16)

            def load_small(g, it, again):
                b0 = it * (NG * GB) + g * GB
                for b in range(GB):
                    if again and b == 0:
                        wait(sp, "y_mm", it - 1, g + 1)
                    sp.dma_start(adjc[g][NS * b:NS * b + NS, :], adj[bass.ds(b0 + b, 1), 0:NS, 0:NS].rearrange("a n d -> (a n) d"))\
                        .then_inc(small_in[g], 16)
                    sp.dma_start(xs[g][NS * b:NS * b + NS, :], x[bass.ds(b0 + b, 1), 0:NS, :].rearrange("a n d -> (a n) d"))\
                        .then_inc(small_in[g], 16)

            def load(g, it, again):
                b0 = it * (NG * GB) + g * GB
                if g:
                    wait(sp, "adj_t", it, g)
                    wait(sp, "deg", it, 3 * g)
                elif again:
                    wait(sp, "adj_t", it - 1, NG)
                    wait(sp, "deg", it - 1, 3 * NG)
                sp.dma_start(adjn[g][:, :, :], ar[:, bass.ds(b0, GB), :]).then_inc(adj_in[g], 16)
                if again:
                    wait(sp, "x1", it - 1, g + 1)
                sp.dma_start(xin[g][:, :, :], xr[:, bass.ds(b0, GB), :]).then_inc(x_in[g], 16)

            def load_again(g, it, again):
                b0 = it * (NG * GB) + g * GB
                if again:
                    wait_g(sp, "a_bin", g, it - 1, 1)
                sp.dma_start(adjr[g][:, :, :], ar[:, bass.ds(b0, GB), :]).then_inc(adjr_in[g], 16)

            def spread_keys(g, it):
                wait(sp, "k_t", it, g + 1)
                for h in range(HEADS):
                    r = slice(DH * h, DH * h + DH)
                    sp.dma_start(km[g][r, :, h, :], kT[g][r, :, :]).then_inc(km_in[g], 16)

            def store(g, it):
                b0 = it * (NG * GB) + g * GB
                wait_g(sp, "x4", g, it, 1)
                sp.dma_start(outr[:, bass.ds(b0, GB), :], x4[g][:, :, :]).then_inc(out_done[g], 16)

            ORDER = [(0, 0, "small"), (1, 0, "keys"), (3, 0, "store"), (2, 1, "again"), (0, 0, "load"),
                     (0, 1, "small"), (1, 1, "keys"), (3, 1, "store"), (1, 0, "again"), (0, 1, "load")]

            def iteration(it, some):
                for lag, g, what in ORDER:
                    if some and not 0 <= it - lag < ITERS:
                        continue
                    n = it - lag
                    again = not (some and n == 0)
                    if what == "keys":
                        spread_keys(g, n)
                    elif what == "small":
                        load_small(g, n, again)
                    elif what == "load":
                        load(g, n, again)
                    elif what == "again":
                        load_again(g, n, again)
                    else:
                        store(g, n)

            for g in range(NG):
                sp.sem_inc(out_done[g], 16)
            for it in range(LAG):
                iteration(it, True)
            with sp.Fori(LAG, ITERS) as it:
                iteration(it, False)
            for it in range(ITERS, ITERS + LAG + 1):
                iteration(it, True)
            for g in range(NG):
                sp.wait_ge(out_done[g], 16 * (ITERS + 1))

        @block.gpsimd
        def _(pool):
            n = [0]

            def after(ins):
                n[0] += 1
                ins.then_inc(w_pool, 1)
                pool.wait_ge(w_pool, n[0])

            after(pool.memset(stage[:, BIAS, :], 0.0))
            after(pool.memset(ident[:, :], 0.0))
            after(pool.affine_select(out=ident[:, :], in_=ident[:, :], compare_op=ALU.not_equal, fill=1.0,
                                     base=0, pattern=[[-1, P]], channel_multiplier=1))
            after(pool.memset(member[:, :, :], 0.0))
            for c, nodes in enumerate(GROUPS):
                a = 0
                while a < len(nodes):
                    b = a
                    while b + 1 < len(nodes) and nodes[b + 1] == nodes[b] + 1:
                        b += 1
                    pool.memset(member[:, c, nodes[a]:nodes[b] + 1], 1.0)
                    a = b + 1
            for t in (nat, hid_t, vp[0], km[0]):
                after(pool.memset(t[tuple([slice(None)] * len(t.shape))], 0.0))
            pool.memset(vp[0][:, :, :, DH:DH + 1], 1.0)
            pool.memset(half_neg[:, :], -0.5).then_inc(consts_ready, 1)

            def root(v, r):
                return pool.tensor_tensor(r[:, :], v[:, :], half_neg[:, 0:GB], ALU.pow)

            def steps(it, g, kind, k):
                if kind == "l0_deg":
                    wait(pool, "l0_prep", it, 10 * g + 5)
                    pool.tensor_tensor(pow0[:, :], deg0_s[:, :], half_neg[:, :], ALU.pow).then_inc(S["l0_pow"], 1)
                elif kind == "l0_add":
                    wait(pool, "ln1", it, 3 * g + 3)
                    root(ve[g][0], rs[g][0]).then_inc(S["ln1_pow"], 1)
                elif kind == "adj_t":
                    wait(pool, "deg", it, 3 * g + 3)
                    root(deg_s[g], deg_p[g]).then_inc(S["deg_pow"], 1)
                elif kind == "te":
                    wait(pool, "adj_t", it, g + 1)
                    passed(pool)
                    pool.tensor_scalar(cols(adjTe[g]), cols(adjT[g]), 1.0, ADJ_EPS, ALU.mult, ALU.add).then_inc(S["adj_te"], 1)
                elif kind == "x1_t":
                    wait(pool, "x1", it, g + 1)
                    wait_before(pool, "y2", it, g)
                    pool.tensor_tensor(x1b[g][:, :, :], x1[g][:, :, :], bo_row[:, :].unsqueeze(1).broadcast_to([P, GB, P]), ALU.add)\
                        .then_inc(S["x1_b"], 1)
                elif kind == "wo" and k == 1:
                    wait(pool, "ln2", it, 3 * g + 3)
                    root(ve[g][1], rs[g][1]).then_inc(S["ln2_pow"], 1)
                elif kind == "l2_t":
                    wait(pool, "t_b", it, g + 1)
                    wait(pool, "dinv", it, g + 1)
                    pool.tensor_tensor(t_d[:, :, :], t_b[:, :, :], per_graph(dinv[g][:, :]), ALU.mult).then_inc(S["t_d"], 1)
                elif kind == "l2_agg":
                    wait(pool, "ln3", it, 3 * g + 3)
                    root(ve[g][2], rs[g][2]).then_inc(S["ln3_pow"], 1)
                elif kind == "begin" or (kind == "turn" and k):
                    wait_g(pool, "h_hi", g, it, k + 1)
                    pool.tensor_tensor(h_lo[g][:, :], hT[g][:, :], h_hi[g][:, :], ALU.subtract).then_inc(SG["h_lo"][g], 1)
                elif kind == "z":
                    wait_g(pool, "n_act", g, it, k + 1)
                    pool.tensor_tensor(hd[g][:, :], hT[g][:, :], nn[g][:, :], ALU.subtract).then_inc(SG["hd"][g], 1)
                elif kind == "end":
                    wait_g(pool, "ln4", g, it, 3)
                    root(ve4[g], rs4[g]).then_inc(SG["ln4_pow"][g], 1)

            program(pool, "gpsimd", steps)

        @block.scalar
        def _(act):
            act.wait_ge(w_prep, 2)
            act.activation(fw[:, :], fwx[:, :], ACT.Exp).then_inc(w_exp, 1)
            act.wait_ge(w_evac, 7)

            def steps(it, g, kind, k):
                n = GB * g + k
                if kind == "l0_y":
                    wait(act, "y_mm", it, g + 1)
                    act.activation(y_t[:, :, :, :].rearrange("p k b n -> p (k b n)"), M2[:, 0:NK * GB * NN], ACT.Copy).then_inc(S["y_t"], 1)
                elif kind == "l0_hid":
                    wait(act, "w1_mm", it, 2 * g + k + 1)
                    for c in range(NK):
                        ins = act.activation(hid_t[:, k, c, :, 0:NN],
                                             M2[:, c * GB * NN:(c + 1) * GB * NN].rearrange("p (b n) -> p b n", b=GB),
                                             ACT.Relu, bias=b1c[:, c, k:k + 1])
                    ins.then_inc(S["hid_t"], 1)
                elif kind == "l0_z" and k == 0:
                    wait(act, "z_mm", it, 2 * g + 1)
                    act.activation(z_s[:, 0:GB, :].rearrange("p k d -> p (k d)"), M2[:, :], ACT.Copy).then_inc(S["z_lo"], 1)
                elif kind == "l0_z":
                    wait(act, "z_mm", it, 2 * g + 2)
                    act.activation(z_s[:, NK - 1, :], M2[:, 0:P], ACT.Copy).then_inc(S["z_hi"], 1)
                elif kind == "l0_out":
                    wait(act, "o_mm", it, g + 1)
                    for c in range(NK):
                        ins = act.activation(o_r[:, c, :, :].rearrange("p b n -> p (b n)"), M2[:, c * GB * NN:(c + 1) * GB * NN],
                                             ACT.Relu, bias=fusion_b2[:, c:c + 1], scale=fusion[:, c:c + 1])
                    ins.then_inc(S["o_relu"], 1)
                elif kind == "adj_t":
                    wait(act, "adjt_mm", it, g + 1)
                    act.activation(cols(adjT[g]), M2[:, :], ACT.Copy).then_inc(S["adj_t"], 1)
                elif kind == "x1_t":
                    wait(act, "x1t_mm", it, g + 1)
                    act.activation(cols(xT[g]), M0[:, :], ACT.Copy).then_inc(S["x1_t"], 1)
                elif kind == "qkv":
                    wait(act, "k_mm", it, g + 1)
                    act.activation(cols(kT[g]), S0[:, :], ACT.Copy).then_inc(S["k_t"], 1)
                    wait(act, "q_mm", it, g + 1)
                    act.activation(cols(qT[g]), S1[:, :], ACT.Copy).then_inc(S["q_t"], 1)
                elif kind == "max":
                    wait(act, "s_neg", it, n + 1)
                    for h in range(HEADS):
                        S_ = S0 if h < GB else S1
                        ins = act.activation(e_s[:, h, :], S_[:, (h % GB) * P:(h % GB + 1) * P], ACT.Exp,
                                             bias=s_ng[:, h:h + 1], scale=SCALE)
                        if h % GB == GB - 1:
                            ins.then_inc(S["e_act"], 1)
                elif kind == "a" and k % 2:
                    wait(act, "av_mm", it, n + 1)
                    act.activation(o_ts[:, :, :, :].rearrange("p a h q -> p (a h q)"), M0[:, :], ACT.Copy).then_inc(S["o_t"], 1)
                elif kind == "on":
                    wait(act, "ont_mm", it, 2 * g + k + 1)
                    act.activation(on_ts[:, :, :].rearrange("p a q -> p (a q)"), M0[:, 0:2 * P], ACT.Copy).then_inc(S["on_t"], 1)
                elif kind == "x2_t":
                    wait(act, "x2t_mm", it, g + 1)
                    act.activation(cols(x2T[g]), M2[:, :], ACT.Copy).then_inc(S["x2_t"], 1)
                elif kind == "begin":
                    wait_g(act, "x3t_mm", g, it, 1)
                    act.activation(hT[g][:, :], RT[:, :], ACT.Copy).then_inc(SG["h_first"][g], 1)
                    wait_g(act, "h_first", g, it, 1)
                    act.activation(h_hi[g][:, :], hT[g][:, :], ACT.Copy).then_inc(SG["h_hi"][g], 1)
                elif kind == "turn" and k:
                    wait_g(act, "h_mm", g, it, k)
                    act.activation(cols(h_tok[g]), RT[:, :], ACT.Copy).then_inc(SG["h_tok"][g], 1)
                    wait_g(act, "h_new", g, it, k)
                    act.activation(h_hi[g][:, :], hT[g][:, :], ACT.Copy).then_inc(SG["h_hi"][g], 1)
                elif kind == "agg":
                    wait_g(act, "agg_mm", g, it, k + 1)
                    act.activation(agg_hi[g][:, :], RT[:, :], ACT.Copy).then_inc(SG["agg_hi"][g], 1)
                elif kind == "r":
                    wait_g(act, "r_mm", g, it, k + 1)
                    act.activation(tr[g][:, :], RA[:, :], ACT.Tanh, bias=b_rz[:, 0:1], scale=0.5).then_inc(SG["r_act"][g], 1)
                elif kind == "hn":
                    wait_g(act, "hn_mm", g, it, k + 1)
                    act.activation(un[g][:, :], RB[:, :], ACT.Identity, bias=b_hn[:, 0:1]).then_inc(SG["u_act"][g], 1)
                elif kind == "in":
                    wait_g(act, "rw", g, it, k + 1)
                    act.activation(nn[g][:, :], tr[g][:, :], ACT.Tanh, bias=bih[:, 2:3]).then_inc(SG["n_act"][g], 1)
                elif kind == "z":
                    wait_g(act, "zg_mm", g, it, k + 1)
                    act.activation(tz[g][:, :], RB[:, :], ACT.Tanh, bias=b_rz[:, 1:2], scale=0.5).then_inc(SG["z_act"][g], 1)

            program(act, "scalar", steps)

        @block.vector
        def _(dve):
            n = [0]

            def after(ins):
                n[0] += 1
                ins.then_inc(w_prep, 1)
                dve.wait_ge(w_prep, n[0])

            dve.wait_ge(w_in, 16 * WEIGHT_DMAS)
            after(dve.tensor_reduce(fw_s[:, 0:1], fw[:, :], AX_X, ALU.max))
            after(dve.tensor_scalar(fwx[:, :], fw[:, :], fw_s[:, 0:1], None, ALU.subtract))
            dve.wait_ge(w_exp, 1)
            after(dve.tensor_reduce(fw_s[:, 1:2], fw[:, :], AX_X, ALU.add))
            after(dve.reciprocal(fw_s[:, 2:3], fw_s[:, 1:2]))
            after(dve.tensor_scalar(fusion[:, :], fw[:, :], fw_s[:, 2:3], None, ALU.mult))
            dve.wait_ge(consts_ready, 1)
            after(dve.tensor_reduce(ident_small[:, :], ident[:, :].rearrange("p (b n) -> p n b", b=GB), AX_X, ALU.add))
            after(dve.tensor_tensor(member_x[:, :, :], member[:, :, :],
                                    ident_small[:, :].unsqueeze(1).broadcast_to([P, NK, NS]), ALU.mult))
            after(dve.tensor_reduce(member_p[:, :], member_x[:, :, :], AX_X, ALU.add))
            banks = [S0, S1, M0, M1, RT]
            for i in range(5):
                dve.wait_ge(w_mm, i + 1)
                m = min(4, 18 - 4 * i)
                dve.tensor_copy(wT[:, 4 * i:4 * i + m, :].rearrange("p a b -> p (a b)"), banks[i][:, 0:m * P]).then_inc(w_evac, 1)
            dve.wait_ge(w_evac, 5)
            after(dve.tensor_tensor(b_rz[:, :], bih, bhh, ALU.add))
            after(dve.tensor_scalar(b_rz[:, :], b_rz[:, :], 0.5, None, ALU.mult))
            after(dve.tensor_scalar(b_hn[:, :], bhh[:, 2:3], 0.5, None, ALU.mult))
            after(dve.tensor_tensor(fusion_b2[:, :], fusion[:, :], b2c, ALU.mult))
            after(dve.tensor_scalar(wT[:, WHH + 2, :], wT[:, WHH + 2, :], 0.5, None, ALU.mult))
            after(dve.tensor_copy(whh_hi[:, :, :], wT[:, WHH:WHH + 3, :]))
            dve.tensor_tensor(whh_lo[:, :, :], wT[:, WHH:WHH + 3, :], whh_hi[:, :, :], ALU.subtract).then_inc(w_evac, 1)
            for i in range(LAYERS):
                dve.wait_ge(w_mm, 6 + i)
                product = [RA, RB, M2, S0, S1][i][:, 0:3 * P]
                after(dve.tensor_copy(comp_hi[:, i, :], product))
                ins = dve.tensor_tensor(comp_lo[:, i, :], product, comp_hi[:, i, :], ALU.subtract)
            ins.then_inc(w_evac, 1)

            def moments(at, y, st, m, v):
                for b in range(GB):
                    ins = dve.bn_stats(st[:, b, :], y[:, b, :])
                at(ins, 1)
                passed(dve)
                for b in range(GB):
                    ins = dve.bn_aggr(m[:, b, :], st[:, b, :])
                at(ins, 2)
                at(dve.tensor_scalar(v[:, :], m[:, :, 1], LN_EPS, None, ALU.add), 3)

            def front_norm(it, g, j, y):
                name = f"ln{j}"

                def at(ins, k):
                    ins.then_inc(S[name], 1)
                    if k < 3:
                        wait(dve, name, it, 3 * g + k)

                moments(at, y, stats[j - 1], mv[g][j - 1], ve[g][j - 1])

            def last_norm(it, g):
                def at(ins, k):
                    ins.then_inc(SG["ln4"][g], 1)
                    if k < 3:
                        wait_g(dve, "ln4", g, it, k)

                moments(at, y4[g], stats4[g], mv4[g], ve4[g])

            def normalise(o, y, m, r):
                for b in range(GB):
                    ins = dve.tensor_scalar(o[:, b, :], y[:, b, :], m[:, b, 0:1], r[:, b:b + 1], ALU.subtract, ALU.mult)
                return ins

            def steps(it, g, kind, k):
                n = GB * g + k
                if kind in ("l0_deg", "l0_prep"):
                    done = [10 * g + (5 if kind == "l0_prep" else 0)]

                    def then(ins):
                        done[0] += 1
                        ins.then_inc(S["l0_prep"], 1)
                        wait(dve, "l0_prep", it, done[0])

                if kind == "l0_deg":
                    dve.wait_ge(small_in[g], (it + 1) * (16 * 2 * GB))
                    then(dve.tensor_tensor(a_i[:, :], adjc[g][:, :], ident_small[:, :], ALU.add))
                    then(dve.tensor_tensor(a_m[:, :, :], member[:, :, :], a_i[:, :].unsqueeze(1).broadcast_to([P, NK, NS]), ALU.mult))
                    then(dve.tensor_reduce(deg0[:, :], a_m[:, :, :], AX_X, ALU.add))
                    then(dve.tensor_scalar(deg0_z[:, :], deg0[:, :], 0.0, None, ALU.is_equal))
                    then(dve.tensor_tensor(deg0_s[:, :], deg0[:, :], deg0_z[:, :], ALU.add))
                elif kind == "l0_prep":
                    wait(dve, "l0_pow", it, g + 1)
                    then(dve.scalar_tensor_tensor(dinv0[:, :], deg0[:, :], 0.0, pow0[:, :], ALU.not_equal, ALU.mult))
                    then(dve.tensor_tensor(dinv0m[:, :], dinv0[:, :], member_p[:, :], ALU.mult))
                    then(dve.tensor_tensor(a_row[:, :, :], a_i[:, :].unsqueeze(1).broadcast_to([P, NK, NS]),
                                           dinv0m[:, :].unsqueeze(2).broadcast_to([P, NK, NS]), ALU.mult))
                    then(dve.transpose(a_col[:, :, :].rearrange("p k n -> p (k n)"), a_row[:, :, :].rearrange("p k n -> p (k n)")))
                    for q in range(GB):
                        r = slice(NS * q, NS * q + NS)
                        ins = dve.tensor_tensor(nat[r, :, q, :], a_col[r, :, 0:NN],
                                                dinv0m[r, :].unsqueeze(2).broadcast_to([NS, NK, NN]), ALU.mult)
                    then(ins)
                elif kind == "l0_fuse":
                    wait(dve, "o_relu", it, g + 1)
                    dve.tensor_tensor(o_m[:, :, :, :], o_r[:, :, :, :],
                                      member[:, :, 0:NN].unsqueeze(2).broadcast_to([P, NK, GB, NN]), ALU.mult).then_inc(S["fused"], 1)
                    wait(dve, "fused", it, 2 * g + 1)
                    dve.tensor_reduce(f_t[:, :], o_m[:, :, :, :].rearrange("p k b n -> p (b n) k"), AX_X, ALU.add)\
                        .then_inc(S["fused"], 1)
                elif kind == "l0_add":
                    dve.wait_ge(x_in[g], (it + 1) * 16)
                    wait(dve, "fused_mm", it, g + 1)
                    dve.tensor_tensor(xin[g][0:NN, :, :].rearrange("p b d -> p (b d)"), M2[0:NN, :],
                                      xin[g][0:NN, :, :].rearrange("p b d -> p (b d)"), ALU.add).then_inc(S["y1"], 1)
                    wait(dve, "y1", it, g + 1)
                    front_norm(it, g, 1, xin[g])
                elif kind == "adj_t":
                    dve.wait_ge(adj_in[g], (it + 1) * 16)
                    dve.tensor_reduce(deg[g][:, :], adjn[g][:, :, :], AX_X, ALU.add).then_inc(S["deg"], 1)
                    wait(dve, "deg", it, 3 * g + 1)
                    dve.tensor_scalar(deg_z[g][:, :], deg[g][:, :], 0.0, None, ALU.is_equal).then_inc(S["deg"], 1)
                    wait(dve, "deg", it, 3 * g + 2)
                    dve.tensor_tensor(deg_s[g][:, :], deg[g][:, :], deg_z[g][:, :], ALU.add).then_inc(S["deg"], 1)
                elif kind == "x1":
                    wait(dve, "ln1_pow", it, g + 1)
                    wait_before(dve, "x1t_mm", it, g)
                    wait_before(dve, "x1_b", it, g)
                    normalise(x1[g], xin[g], mv[g][0], rs[g][0]).then_inc(S["x1"], 1)
                elif kind == "x2":
                    wait(dve, "ln2_pow", it, g + 1)
                    normalise(x2[g], y2[g], mv[g][1], rs[g][1]).then_inc(S["x2"], 1)
                    wait(dve, "deg_pow", it, g + 1)
                    dve.scalar_tensor_tensor(dinv[g][:, :], deg[g][:, :], 0.0, deg_p[g][:, :], ALU.not_equal, ALU.mult)\
                        .then_inc(S["dinv"], 1)
                elif kind == "qkv":
                    wait(dve, "v_mm", it, g + 1)
                    dve.tensor_copy(vp[g][:, :, :, 0:DH], M1[:, :].rearrange("p (b h d) -> p b h d", b=GB, h=HEADS))\
                        .then_inc(S["v_p"], 1)
                elif kind == "max":
                    wait(dve, "s_mm", it, n + 1)
                    dve.tensor_reduce(s_mx[:, 0:GB], S0[:, :].rearrange("p (h k) -> p h k", h=GB), AX_X, ALU.max)
                    dve.tensor_reduce(s_mx[:, GB:HEADS], S1[:, :].rearrange("p (h k) -> p h k", h=GB), AX_X, ALU.max)\
                        .then_inc(S["s_max"], 1)
                    wait(dve, "s_max", it, n + 1)
                    dve.tensor_scalar(s_ng[:, :], s_mx[:, :], -SCALE, None, ALU.mult).then_inc(S["s_neg"], 1)
                elif kind == "p":
                    wait(dve, "adj_te", it, g + 1)
                    for j, S_ in enumerate((S0, S1)):
                        wait(dve, "et_mm", it, 2 * n + j + 1)
                        dve.tensor_tensor(p_s[:, GB * j:GB * j + GB, :], S_[:, :].rearrange("p (h q) -> p h q", h=GB),
                                          adjTe[g][:, k, :].unsqueeze(1).broadcast_to([P, GB, P]), ALU.mult).then_inc(S["p_t"], 1)
                elif kind == "u":
                    wait(dve, "u_mm", it, 2 * g + k + 1)
                    o4 = M1[:, :].rearrange("p (a h d) -> p a h d", a=2, h=HEADS)
                    dve.reciprocal(den[:, :, :], o4[:, :, :, DH]).then_inc(S["den"], 1)
                    wait(dve, "den", it, 2 * g + k + 1)
                    dve.tensor_tensor(o_ns[:, :, :, :], o4[:, :, :, 0:DH],
                                      den[:, :, :].unsqueeze(3).broadcast_to([P, 2, HEADS, DH]), ALU.mult).then_inc(S["o_n"], 1)
                elif kind == "wo":
                    wait(dve, "x1_b", it, g + 1)
                    wait(dve, "wo_mm", it, 2 * g + k + 1)
                    dve.tensor_tensor(y2[g][:, 2 * k:2 * k + 2, :].rearrange("p a d -> p (a d)"), M1[:, 0:2 * P],
                                      x1b[g][:, 2 * k:2 * k + 2, :].rearrange("p a d -> p (a d)"), ALU.add).then_inc(S["y2"], 1)
                    if k == 1:
                        wait(dve, "y2", it, 2 * g + 2)
                        front_norm(it, g, 2, y2[g])
                elif kind == "l2_t":
                    wait(dve, "t_mm", it, g + 1)
                    dve.tensor_tensor(t_b[:, :, :], M2[:, :].rearrange("p (b d) -> p b d", b=GB),
                                      l2b_row[:, :].unsqueeze(1).broadcast_to([P, GB, P]), ALU.add).then_inc(S["t_b"], 1)
                elif kind == "l2_agg":
                    wait(dve, "a_mm", it, g + 1)
                    wait(dve, "x2", it, g + 1)
                    dve.scalar_tensor_tensor(a_r[:, :, :], M2[:, :].rearrange("p (b d) -> p b d", b=GB), 0.0,
                                             per_graph(dinv[g][:, :]), ALU.max, ALU.mult).then_inc(S["a_relu"], 1)
                    wait(dve, "a_relu", it, g + 1)
                    dve.tensor_tensor(cols(y3[g]), cols(a_r), cols(x2[g]), ALU.add).then_inc(S["y3"], 1)
                    wait(dve, "y3", it, g + 1)
                    front_norm(it, g, 3, y3[g])
                elif kind == "bin":
                    dve.wait_ge(adjr_in[g], (it + 1) * 16)
                    dve.tensor_scalar(cols(a_bin[g]), cols(adjr[g]), 0.0, None, ALU.not_equal).then_inc(SG["a_bin"][g], 1)
                elif kind == "x3":
                    wait(dve, "ln3_pow", it, g + 1)
                    normalise(x3[g], y3[g], mv[g][2], rs[g][2]).then_inc(SG["x3"][g], 1)
                elif kind == "agg_lo":
                    wait_g(dve, "agg_hi", g, it, k + 1)
                    dve.tensor_tensor(agg_lo[g][:, :], RT[:, :], agg_hi[g][:, :], ALU.subtract).then_inc(SG["agg_t"][g], 1)
                elif kind == "hn":
                    wait_g(dve, "r_act", g, it, k + 1)
                    wait_g(dve, "u_act", g, it, k + 1)
                    dve.scalar_tensor_tensor(un[g][:, :], tr[g][:, :], 1.0, un[g][:, :], ALU.add, ALU.mult).then_inc(SG["rv"][g], 1)
                elif kind == "in":
                    wait_g(dve, "rv", g, it, k + 1)
                    wait_g(dve, "in_mm", g, it, k + 1)
                    dve.tensor_tensor(tr[g][:, :], RA[:, :], un[g][:, :], ALU.add).then_inc(SG["rw"][g], 1)
                elif kind == "h_new":
                    wait_g(dve, "hd", g, it, k + 1)
                    wait_g(dve, "z_act", g, it, k + 1)
                    dve.scalar_tensor_tensor(hd[g][:, :], tz[g][:, :], 1.0, hd[g][:, :], ALU.add, ALU.mult).then_inc(SG["he"][g], 1)
                    wait_g(dve, "he", g, it, k + 1)
                    dve.scalar_tensor_tensor(hT[g][:, :], hd[g][:, :], 0.5, nn[g][:, :], ALU.mult, ALU.add).then_inc(SG["h_new"][g], 1)
                elif kind == "end":
                    wait_g(dve, "f_mm", g, it, 1)
                    for b in range(GB):
                        in_graph = wT[:, MASK, bass.ds(it * (NG * GB) + g * GB + b, 1)]
                        ins = dve.scalar_tensor_tensor(y4[g][:, b, :], RT[:, b * P:(b + 1) * P], in_graph,
                                                       x3[g][:, b, :], ALU.mult, ALU.add)
                    ins.then_inc(SG["y4"][g], 1)
                    wait_g(dve, "y4", g, it, 1)
                    last_norm(it, g)
                elif kind == "out":
                    wait_g(dve, "ln4_pow", g, it, 1)
                    dve.wait_ge(out_done[g], (it + 1) * 16)
                    normalise(x4[g], y4[g], mv4[g], rs4[g]).then_inc(SG["x4"][g], 1)

            program(dve, "vector", steps)

        @block.tensor
        def _(pe):
            def turn(o, i, rows=P):
                return pe.transpose(o, i, ident[0:rows, 0:rows])

            pe.wait_ge(consts_ready, 1)
            pe.wait_ge(w_in, 16 * WEIGHT_DMAS)
            banks = [S0, S1, M0, M1, RT]
            for i in range(18):
                ins = turn(banks[i // 4][:, (i % 4) * P:(i % 4 + 1) * P], stage[:, i, :])
                if i % 4 == 3 or i == 17:
                    ins.then_inc(w_mm, 1)
            pe.wait_ge(w_evac, 5)
            for i in range(LAYERS):
                pe.matmul([RA, RB, M2, S0, S1][i][:, 0:3 * P], wT[:, WL + i, :], wT[:, WIH:WIH + 3, :].rearrange("p c f -> p (c f)"),
                          start=True, stop=True).then_inc(w_mm, 1)
            pe.wait_ge(w_evac, 7)

            def gate(o, l, c, w, g, last, it=None):
                pairs = []
                if w is not None:
                    pairs += [(whh_hi[:, w, :], h_hi[g]), (whh_hi[:, w, :], h_lo[g]), (whh_lo[:, w, :], h_hi[g])]
                if c is not None:
                    hi, lo = comp_hi[:, l, c * P:(c + 1) * P], comp_lo[:, l, c * P:(c + 1) * P]
                    pairs += [(hi, agg_hi[g]), (lo, agg_hi[g]), (hi, agg_lo[g])]
                for i, (weights, moving) in enumerate(pairs):
                    if last == "r_mm" and i == 3:
                        wait_g(pe, "agg_hi", g, it, l + 1)
                    elif last == "r_mm" and i == 5:
                        wait_g(pe, "agg_t", g, it, l + 1)
                    ins = pe.matmul(o[:, :], weights, moving[:, :], start=i == 0, stop=i == len(pairs) - 1)
                ins.then_inc(SG[last][g], 1)

            def slot_before(name, it, g, k):
                g2, k2 = BEFORE[g, k]
                back = LAG_OF[g2, k2] - LAG_OF[g, k] + (SLOTS.index((g, k)) == 0)
                if not (isinstance(it, int) and not 0 <= it - back < ITERS):
                    wait_g(pe, name, g2, it - back, k2 + 1)

            def steps(it, g, kind, k):
                n = GB * g + k
                if kind == "l0_y":
                    wait(pe, "l0_prep", it, 10 * g + 10)
                    pe.wait_ge(small_in[g], (it + 1) * (16 * 2 * GB))
                    if not (isinstance(it, int) and it + g == 0):
                        wait(pe, "y1", it + g - 1, 2 - g)
                    pe.matmul(M2[:, 0:NK * GB * NN], xs[g][:, :], nat[:, :, :, :].rearrange("p k b n -> p (k b n)"),
                              start=True, stop=True).then_inc(S["y_mm"], 1)
                elif kind == "l0_hid":
                    if k == 0:
                        wait(pe, "y_t", it, g + 1)
                    else:
                        wait(pe, "hid_t", it, 2 * g + 1)
                    for c in range(NK):
                        ins = pe.matmul(M2[:, c * GB * NN:(c + 1) * GB * NN], W1s[:, c, k * P:(k + 1) * P],
                                        y_t[:, c, :, :].rearrange("p b n -> p (b n)"), start=True, stop=True)
                    ins.then_inc(S["w1_mm"], 1)
                elif kind == "l0_z":
                    if k == 0:
                        wait(pe, "hid_t", it, 2 * g + 2)
                    else:
                        wait(pe, "z_lo", it, g + 1)
                    for c in (range(GB) if k == 0 else [NK - 1]):
                        for h in range(2):
                            ins = pe.matmul(M2[:, (c % GB) * P:(c % GB + 1) * P], hid_t[:, h, c, :, :].rearrange("p b n -> p (b n)"),
                                            W2s[:, c, h, :], start=(h == 0), stop=(h == 1))
                    ins.then_inc(S["z_mm"], 1)
                elif kind == "l0_out":
                    wait(pe, "z_hi", it, g + 1)
                    for c in range(NK):
                        ins = pe.matmul(M2[:, c * GB * NN:(c + 1) * GB * NN], z_s[:, c, :],
                                        nat[:, c, :, :].rearrange("p b n -> p (b n)"), start=True, stop=True)
                    ins.then_inc(S["o_mm"], 1)
                elif kind == "adj_t":
                    pe.wait_ge(adj_in[g], (it + 1) * 16)
                    if isinstance(it, int) and it == 0:
                        wait(pe, "o_relu", it, g + 1)
                    else:
                        wait(pe, "a_relu", it - 1, g + 1)
                    for q in range(GB):
                        ins = turn(M2[:, q * P:(q + 1) * P], adjn[g][:, q, :])
                    ins.then_inc(S["adjt_mm"], 1)
                elif kind == "l0_add":
                    wait(pe, "fused", it, 2 * g + 2)
                    wait(pe, "adj_t", it, g + 1)
                    for q in range(GB):
                        ins = pe.matmul(M2[0:NN, q * P:(q + 1) * P], f_t[:, q * NN:(q + 1) * NN], ident[:, :], start=True, stop=True)
                    ins.then_inc(S["fused_mm"], 1)
                elif kind == "x1_t":
                    wait(pe, "x1", it, g + 1)
                    wait_before(pe, "on_t", it, g)
                    for q in range(GB):
                        ins = turn(M0[:, q * P:(q + 1) * P], x1[g][:, q, :])
                    ins.then_inc(S["x1t_mm"], 1)
                elif kind == "qkv":
                    wait(pe, "x1_t", it, g + 1)
                    pe.matmul(S0[:, :], wT[:, WK, :], cols(xT[g]), start=True, stop=True).then_inc(S["k_mm"], 1)
                    pe.matmul(S1[:, :], wT[:, WQ, :], cols(xT[g]), start=True, stop=True).then_inc(S["q_mm"], 1)
                    wait_before(pe, "y2", it, g)
                    for q in range(GB):
                        ins = pe.matmul(M1[:, q * P:(q + 1) * P], xT[g][:, q, :], wT[:, WV, :], start=True, stop=True)
                    ins.then_inc(S["v_mm"], 1)
                elif kind == "s":
                    if k == 0:
                        wait(pe, "k_t", it, g + 1)
                        wait(pe, "q_t", it, g + 1)
                        pe.wait_ge(km_in[g], (it + 1) * (16 * HEADS))
                    else:
                        wait(pe, "p_t", it, 2 * n)
                    for j, S_ in enumerate((S0, S1)):
                        ins = pe.matmul(S_[:, :], qT[g][:, k, :], km[g][:, k, GB * j:GB * j + GB, :].rearrange("p h k -> p (h k)"),
                                        start=True, stop=True)
                    ins.then_inc(S["s_mm"], 1)
                elif kind == "t":
                    for j, S_ in enumerate((S0, S1)):
                        wait(pe, "e_act", it, 2 * n + j + 1)
                        for h in range(GB):
                            ins = turn(S_[:, h * P:(h + 1) * P], e_s[:, GB * j + h, :])
                        ins.then_inc(S["et_mm"], 1)
                elif kind == "a":
                    if k == 0:
                        wait(pe, "v_p", it, g + 1)
                    if k == 2:
                        wait(pe, "on_t", it, 2 * g + 1)
                    for h in range(HEADS):
                        wait(pe, "p_t", it, 2 * n + h // GB + 1) if h % GB == 0 else None
                        c = (k % 2) * 2 * P + (h // GB) * P
                        r = NS * (h % GB)
                        ins = pe.matmul(M0[r:r + NS, c:c + P], vp[g][:, k, h, :], p_s[:, h, :], start=True, stop=True)
                    ins.then_inc(S["av_mm"], 1)
                elif kind == "u":
                    wait(pe, "o_t", it, 2 * g + k + 1)
                    if k == 0:
                        wait(pe, "v_p", it, g + 1)
                    else:
                        wait(pe, "y2", it, 2 * g + 1)
                    for j in range(4):
                        ins = turn(M1[:, j * P:(j + 1) * P], o_ts[:, j // 2, j % 2, :])
                    ins.then_inc(S["u_mm"], 1)
                elif kind == "on":
                    wait(pe, "o_n", it, 2 * g + k + 1)
                    for j in range(2):
                        ins = turn(M0[:, j * P:(j + 1) * P], o_ns[:, j, :, :].rearrange("p h d -> p (h d)"))
                    ins.then_inc(S["ont_mm"], 1)
                elif kind == "wo":
                    wait(pe, "on_t", it, 2 * g + k + 1)
                    for j in range(2):
                        ins = pe.matmul(M1[:, j * P:(j + 1) * P], on_ts[:, j, :], wT[:, WO, :], start=True, stop=True)
                    ins.then_inc(S["wo_mm"], 1)
                elif kind == "x2_t":
                    wait(pe, "x2", it, g + 1)
                    if not (isinstance(it, int) and it + 1 == ITERS):
                        wait(pe, "o_relu", it + 1, g + 1)
                    for q in range(GB):
                        ins = turn(M2[:, q * P:(q + 1) * P], x2[g][:, q, :])
                    ins.then_inc(S["x2t_mm"], 1)
                elif kind == "l2_t":
                    wait(pe, "x2_t", it, g + 1)
                    for q in range(GB):
                        ins = pe.matmul(M2[:, q * P:(q + 1) * P], x2T[g][:, q, :], wT[:, WL2, :], start=True, stop=True)
                    ins.then_inc(S["t_mm"], 1)
                elif kind == "l2_agg":
                    wait(pe, "t_d", it, g + 1)
                    for q in range(GB):
                        ins = pe.matmul(M2[:, q * P:(q + 1) * P], adjT[g][:, q, :], t_d[:, q, :], start=True, stop=True)
                    ins.then_inc(S["a_mm"], 1)
                elif kind == "begin":
                    wait_g(pe, "x3", g, it, 1)
                    if not (isinstance(it, int) and it + g == 0):
                        wait_g(pe, "agg_t", 1 - g, it + g - 1, 3)
                    for q in range(GB):
                        ins = turn(RT[:, q * P:(q + 1) * P], x3[g][:, q, :])
                    ins.then_inc(SG["x3t_mm"][g], 1)
                elif kind == "turn" and k:
                    wait_g(pe, "h_new", g, it, k)
                    slot_before("agg_t", it, g, k)
                    if k == LAYERS - 2 and isinstance(it, int) and it + g > 0:
                        wait_g(pe, "y4", 1 - g, it + g - 1, 1)
                    for q in range(GB):
                        ins = turn(RT[:, q * P:(q + 1) * P], hT[g][:, q * P:(q + 1) * P])
                    ins.then_inc(SG["h_mm"][g], 1)
                elif kind == "agg":
                    if k == 0:
                        wait_g(pe, "a_bin", g, it, 1)
                        wait_g(pe, "h_first", g, it, 1)
                    else:
                        wait_g(pe, "h_tok", g, it, k)
                    src = x3[g] if k == 0 else h_tok[g]
                    for q in range(GB):
                        ins = pe.matmul(RT[:, q * P:(q + 1) * P], src[:, q, :], a_bin[g][:, q, :], start=True, stop=True)
                    ins.then_inc(SG["agg_mm"][g], 1)
                elif kind == "r":
                    wait_g(pe, "h_hi", g, it, k + 1)
                    wait_g(pe, "h_lo", g, it, k + 1)
                    slot_before("rw", it, g, k)
                    gate(RA, k, 0, 0, g, "r_mm", it)
                elif kind == "hn":
                    slot_before("z_act", it, g, k)
                    gate(RB, k, None, 2, g, "hn_mm")
                elif kind == "in":
                    wait_g(pe, "r_act", g, it, k + 1)
                    gate(RA, k, 2, None, g, "in_mm")
                elif kind == "z":
                    wait_g(pe, "u_act", g, it, k + 1)
                    gate(RB, k, 1, 1, g, "zg_mm")
                elif kind == "end":
                    wait_g(pe, "h_new", g, it, LAYERS)
                    if not (isinstance(it, int) and it + g >= ITERS):
                        wait_g(pe, "agg_t", 1 - g, it + g, 3)
                    for q in range(GB):
                        ins = turn(RT[:, q * P:(q + 1) * P], hT[g][:, q * P:(q + 1) * P])
                    ins.then_inc(SG["f_mm"][g], 1)

            program(pe, "tensor", steps)


_INS = ['x', 'adj', 'nodemask', 'L0_gnn_W1', 'L0_gnn_b1', 'L0_gnn_W2', 'L0_gnn_b2', 'L0_gnn_fusion_w', 'L1_gnn_Wq',
        'L1_gnn_Wk', 'L1_gnn_Wv', 'L1_gnn_Wo', 'L1_gnn_bo', 'L2_gnn_W', 'L2_gnn_b', 'L3_gnn_weight', 'L3_gnn_w_ih',
        'L3_gnn_w_hh', 'L3_gnn_b_ih', 'L3_gnn_b_hh']


def kernel(**inputs):
    import numpy as _np
    import concourse.bacc as _bacc
    from concourse import mybir as _mybir
    from concourse.bass_utils import run_bass_kernel_spmd as _run

    nc = _bacc.Bacc("TRN2", target_bir_lowering=False, num_devices=1)
    arrays, args = {}, []
    for name in _INS:
        a = _np.ascontiguousarray(inputs[name])
        arrays[f"in_{name}_dram"] = a
        args.append(nc.dram_tensor(f"in_{name}_dram", a.shape, _mybir.dt.from_np(a.dtype), kind="ExternalInput").ap())
    args.append(nc.dram_tensor("out_0_dram", inputs["x"].shape, _mybir.dt.float32, kind="ExternalOutput").ap())
    gnn_stack_kernel(nc, *args)
    r = _run(nc, [arrays], core_ids=[0])
    return r.results[0]["out_0_dram"]
```
